# Optimizing a Trainium2 kernel written in Bass

```python
import numpy as np
import jax
import jax.numpy as jnp

def _softmax(x, axis=-1):
    return jax.nn.softmax(x, axis=axis)

def _gelu(x):
    return jax.nn.gelu(x, approximate=True)

def _silu(x):
    return jax.nn.silu(x)

def _sigmoid(x):
    return jax.nn.sigmoid(x)

def _layernorm(x, axis=-1, eps=1e-05):
    m = jnp.mean(x, axis=axis, keepdims=True)
    v = jnp.var(x, axis=axis, keepdims=True)
    return (x - m) / jnp.sqrt(v + eps)

def _scatter_add(tgt, idx, src, axis=0):
    return tgt.at[idx].add(src)

def _segment_sum(src, seg, n):
    return jax.ops.segment_sum(src, seg, n)
kernel_name = 'mk_early_fusion_d1_tok_img1024_r4_a6e3a4'

def setup_inputs(seed: int=0):
    np.random.seed(seed)
    _w = jnp.asarray

    def _rec_inputs():
        import jax
        import jax.numpy as jnp
        _rk = jax.random.key(seed)
        x = -0.00016672 + 0.999947 * jax.random.normal(jax.random.fold_in(_rk, 1), (32, 3, 96, 96), jnp.float32)
        txt = 0.00180885 + 1.15405 * jax.random.normal(jax.random.fold_in(_rk, 2), (32, 77, 256), jnp.float32)
        return (x, txt)
    x, txt = _rec_inputs()

    def _L0_tok_setup():
        import jax, jax.numpy as jnp
        import numpy as np
        PATCH = 16

        def _patchify(x, p):
            B, C, H, W = x.shape
            nh, nw = (H // p, W // p)
            x = x.reshape(B, C, nh, p, nw, p)
            x = x.transpose(0, 2, 4, 1, 3, 5)
            return x.reshape(B, nh * nw, C * p * p)
        key = jax.random.key(seed)
        k1, k2, k3, k4, k5 = jax.random.split(key, 5)
        B, C, H = (64, 3, 96)
        d_model = 256
        p = PATCH
        num_patches = (H // p) ** 2
        in_dim = p * p * C
        x = jax.random.normal(k1, (B, C, H, H), dtype=jnp.float32)
        bound = 1.0 / np.sqrt(in_dim)
        W = jax.random.uniform(k2, (d_model, in_dim), dtype=jnp.float32, minval=-bound, maxval=bound)
        b = jax.random.uniform(k3, (d_model,), dtype=jnp.float32, minval=-bound, maxval=bound)
        cls_token = jax.random.normal(k4, (1, 1, d_model), dtype=jnp.float32)
        pos_enc = jax.random.normal(k5, (1, num_patches + 1, d_model), dtype=jnp.float32)
        return {'x': x, 'W': W, 'b': b, 'cls_token': cls_token, 'pos_enc': pos_enc}
    _L0_tok_all = _L0_tok_setup()
    _L0_tok_in = {k: v for k, v in _L0_tok_all.items() if k in ('W', 'b', 'cls_token', 'pos_enc')}
    del _L0_tok_all

    def _L0_attn_setup():
        import jax, jax.numpy as jnp
        import numpy as np
        import math
        D_MODEL = 256
        D_K = 64
        D_V = 64
        N_HEADS = 16
        key = jax.random.key(seed)
        ks = jax.random.split(key, 5)
        std = 1.0 / math.sqrt(D_MODEL)
        x = jax.random.normal(ks[0], (2, 512, D_MODEL), dtype=jnp.float32)
        Wq = jax.random.normal(ks[1], (D_MODEL, N_HEADS * D_K), dtype=jnp.float32) * std
        Wk = jax.random.normal(ks[2], (D_MODEL, N_HEADS * D_K), dtype=jnp.float32) * std
        Wv = jax.random.normal(ks[3], (D_MODEL, N_HEADS * D_V), dtype=jnp.float32) * std
        Wo = jax.random.normal(ks[4], (N_HEADS * D_V, D_MODEL), dtype=jnp.float32) * std
        return {'x': x, 'Wq': Wq, 'Wk': Wk, 'Wv': Wv, 'Wo': Wo}
    _L0_attn_all = _L0_attn_setup()
    _L0_attn_in = {k: v for k, v in _L0_attn_all.items() if k in ('Wq', 'Wk', 'Wv', 'Wo')}
    del _L0_attn_all

    def _L0_ffn_setup():
        import math
        import jax, jax.numpy as jnp
        import numpy as np
        D_MODEL = 256
        D_HIDDEN = 1024
        N_EXPERTS = 8
        TOP_K = 2
        CAPACITY_FACTOR = 1.25
        key = jax.random.key(seed)
        ks = jax.random.split(key, 8)
        s = 0.02
        x = jax.random.normal(ks[0], (4, 512, D_MODEL), dtype=jnp.float32)
        router_w = jax.random.normal(ks[1], (D_MODEL, N_EXPERTS), dtype=jnp.float32) * s
        router_b = jnp.zeros((N_EXPERTS,), dtype=jnp.float32)
        w1 = jax.random.normal(ks[2], (N_EXPERTS, D_MODEL, D_HIDDEN), dtype=jnp.float32) * s
        b1 = jnp.zeros((N_EXPERTS, D_HIDDEN), dtype=jnp.float32)
        w2 = jax.random.normal(ks[3], (N_EXPERTS, D_HIDDEN, D_MODEL), dtype=jnp.float32) * s
        b2 = jnp.zeros((N_EXPERTS, D_MODEL), dtype=jnp.float32)
        return {'x': x, 'router_w': router_w, 'router_b': router_b, 'w1': w1, 'b1': b1, 'w2': w2, 'b2': b2}
    _L0_ffn_all = _L0_ffn_setup()
    _L0_ffn_in = {k: v for k, v in _L0_ffn_all.items() if k in ('router_w', 'router_b', 'w1', 'b1', 'w2', 'b2')}
    del _L0_ffn_all
    return {'x': x, 'txt': txt, 'L0_tok_W': _L0_tok_in['W'], 'L0_tok_b': _L0_tok_in['b'], 'L0_tok_cls_token': _L0_tok_in['cls_token'], 'L0_tok_pos_enc': _L0_tok_in['pos_enc'], 'L0_attn_Wq': _L0_attn_in['Wq'], 'L0_attn_Wk': _L0_attn_in['Wk'], 'L0_attn_Wv': _L0_attn_in['Wv'], 'L0_attn_Wo': _L0_attn_in['Wo'], 'L0_ffn_router_w': _L0_ffn_in['router_w'], 'L0_ffn_router_b': _L0_ffn_in['router_b'], 'L0_ffn_w1': _L0_ffn_in['w1'], 'L0_ffn_b1': _L0_ffn_in['b1'], 'L0_ffn_w2': _L0_ffn_in['w2'], 'L0_ffn_b2': _L0_ffn_in['b2']}

def reference(x, txt, L0_tok_W, L0_tok_b, L0_tok_cls_token, L0_tok_pos_enc, L0_attn_Wq, L0_attn_Wk, L0_attn_Wv, L0_attn_Wo, L0_ffn_router_w, L0_ffn_router_b, L0_ffn_w1, L0_ffn_b1, L0_ffn_w2, L0_ffn_b2):
    import jax
    import jax.numpy as jnp

    def _L0_tok_ref(x, W, b, cls_token, pos_enc):
        import jax, jax.numpy as jnp
        import numpy as np
        PATCH = 16

        def _patchify(x, p):
            B, C, H, W = x.shape
            nh, nw = (H // p, W // p)
            x = x.reshape(B, C, nh, p, nw, p)
            x = x.transpose(0, 2, 4, 1, 3, 5)
            return x.reshape(B, nh * nw, C * p * p)
        B = x.shape[0]
        patches = _patchify(x, PATCH)
        proj = jnp.einsum('bnf,df->bnd', patches, W) + b
        cls = jnp.broadcast_to(cls_token, (B, 1, cls_token.shape[-1]))
        out = jnp.concatenate([cls, proj], axis=1) + pos_enc
        return out

    def _L0_attn_ref(x, Wq, Wk, Wv, Wo):
        import jax, jax.numpy as jnp
        import numpy as np
        import math
        D_MODEL = 256
        D_K = 64
        D_V = 64
        N_HEADS = 16
        B, S, D = x.shape
        H, dk, dv = (N_HEADS, D_K, D_V)
        q = (x @ Wq).reshape(B, S, H, dk)
        k = (x @ Wk).reshape(B, S, H, dk)
        v = (x @ Wv).reshape(B, S, H, dv)
        scores = jnp.einsum('bqhd,bkhd->bhqk', q / math.sqrt(dk), k)
        causal = jnp.tril(jnp.ones((S, S), dtype=bool))
        scores = scores + jnp.where(causal, 0.0, -jnp.inf).astype(scores.dtype)
        attn = jax.nn.softmax(scores, axis=-1)
        out = jnp.einsum('bhqk,bkhd->bqhd', attn, v).reshape(B, S, H * dv)
        return x + out @ Wo

    def _L0_ffn_ref(x, router_w, router_b, w1, b1, w2, b2):
        import math
        import jax, jax.numpy as jnp
        import numpy as np
        D_MODEL = 256
        D_HIDDEN = 1024
        N_EXPERTS = 8
        TOP_K = 2
        CAPACITY_FACTOR = 1.25
        B, T, D = x.shape
        N = B * T
        E = N_EXPERTS
        capacity = max(1, math.ceil(N / E * CAPACITY_FACTOR))
        x_flat = x.reshape(N, D)
        logits = x_flat.astype(jnp.float32) @ router_w + router_b
        gates = jax.nn.softmax(logits, axis=-1)
        _, topk_idx = jax.lax.top_k(gates, TOP_K)
        expert_mask = jax.nn.one_hot(topk_idx, E, dtype=jnp.int32).sum(1)
        pos = jnp.cumsum(expert_mask, axis=0) - 1
        expert_mask = expert_mask * (pos < capacity)
        valid = expert_mask > 0
        pos_c = jnp.where(valid, pos, capacity)
        e_idx = jnp.broadcast_to(jnp.arange(E), (N, E))
        dispatched = x_flat[:, None, :] * valid[:, :, None].astype(x.dtype)
        buf = jnp.zeros((E, capacity + 1, D), x.dtype).at[e_idx.ravel(), pos_c.ravel()].add(dispatched.reshape(N * E, D))
        buf = buf[:, :capacity]
        h = jax.nn.gelu(jnp.einsum('ecd,edh->ech', buf, w1) + b1[:, None, :], approximate=False)
        out = jnp.einsum('ech,ehd->ecd', h, w2) + b2[:, None, :]
        pos_g = jnp.minimum(pos_c, capacity - 1)
        gathered = out[e_idx, pos_g]
        weights = (gates * valid).astype(x.dtype)
        y = jnp.einsum('ned,ne->nd', gathered, weights)
        return y.reshape(B, T, D)
    h = _L0_tok_ref(x, L0_tok_W, L0_tok_b, L0_tok_cls_token, L0_tok_pos_enc)
    h = jnp.concatenate([h, txt], axis=1)
    h = h + _L0_attn_ref(_layernorm(h, axis=-1), L0_attn_Wq, L0_attn_Wk, L0_attn_Wv, L0_attn_Wo)
    h = h + _L0_ffn_ref(_layernorm(h, axis=-1), L0_ffn_router_w, L0_ffn_router_b, L0_ffn_w1, L0_ffn_b1, L0_ffn_w2, L0_ffn_b2)
    return h

_drawn_inputs = setup_inputs


def setup_inputs(seed=0):
    import zlib

    import numpy as np

    out = dict(_drawn_inputs(seed))
    spreads = {'L0_ffn_router_b': (0.0, 0.8), 'L0_ffn_b1': (0.0, 0.8), 'L0_ffn_b2': (0.0, 0.8)}
    factors = {'L0_tok_b': 3.46, 'L0_ffn_router_w': 4.751, 'L0_ffn_w1': 5.834, 'L0_ffn_w2': 5.463}
    for name, (base, spread) in spreads.items():
        noise = np.random.default_rng([zlib.crc32(name.encode()), seed]).standard_normal(out[name].shape)
        drawn = base * np.exp(spread * noise) if base else spread * noise
        out[name] = jnp.asarray(drawn.astype(out[name].dtype))
    for name, factor in factors.items():
        out[name] = (out[name] * factor).astype(out[name].dtype)
    return out
```

```python
from contextlib import ExitStack

import concourse.bass as bass
from concourse import mybir

F32 = mybir.dt.float32
F32R = mybir.dt.float32r
BF16 = mybir.dt.bfloat16
I32 = mybir.dt.int32
ALU = mybir.AluOpType
ACT = mybir.ActivationFunctionType
AX = mybir.AxisListType

B, CH, IMG = 32, 3, 96
PX = 16
NPS = IMG // PX
NP = NPS * NPS
TXT = 77
T = 1 + NP + TXT
D = 256
H, DK = 16, 64
HD = H * DK
E, HID = 8, 1024
TOPK = 2
CAP = -(-B * T * 5 // (4 * E))
EPS = 1e-5
SCALE = DK ** -0.5
NEG = -3.0e38
OUT_OF_RANGE = 16384.0

GB = 4
G = B // GB
GT = GB * T
KC = D // 128
HP = H // 2
PAIRS = HP * GB // 2
PR = CH * PX
HPX = PX // 2
ROW = 272
GATE0, ID = D, D + E
CT = CAP // T
MC = HID // 128
SPLIT_N = (288, CAP - 288)
SLOT_PARTS = ((0, 3), (3, CT - 3))
XJOBS = [(k, part) for k in range(KC) for part in SLOT_PARTS]
EB = 5
ROUTE_PARTS = (2, 5, 5, 6, 5, 5)
ROUTE_STEPS = sum(ROUTE_PARTS)
CONSTS, SMALL = 9, 64
PIX = 16 * 2 * CH * GB
TOKENS = 16 * (2 + GB)
assert CAP == CT * T and GT <= 512 and IMG == NPS * PX


def build(nc, x, txt, tokW, tok_b, cls_token, pos_enc, Wq, Wk, Wv, Wo,
          router_w, router_b, w1, b1, w2, b2, out, slots):
    ctx = ExitStack()
    with ctx:
        def sem(name):
            return ctx.enter_context(nc.semaphore(name))

        base_addr = -(-nc.sbuf_base // 32) * 32
        used = [base_addr]

        def place(name, shape, dt=F32):
            size = 2 if dt == BF16 else 4
            for n in shape[1:]:
                size *= n
            t = nc.alloc_sbuf_tensor_at(name, shape, dt, offset=used[0])
            used[0] += -(-size // 32) * 32
            return t

        ident = place("ident", [128, 128])
        b1T = place("b1T", [128, E * MC])
        stage_a = place("stage_a", [128, 2048])
        stage_b = place("stage_b", [128, 2048])
        neg_half = place("neg_half", [T, GB])
        shared = used[0]

        mask = place("mask", [T, T])
        upto = place("upto", [T, T], BF16)
        ones = place("ones", [T, T], BF16)
        router_sb = place("router_sb", [128, KC, E])
        router_bb = place("router_bb", [T, GB, E])
        io8 = place("io8", [T, GB, E])
        wqkv_hi = place("wqkv_hi", [128, KC, 3 * HD], F32R)
        wqkv_lo = place("wqkv_lo", [128, KC, 3 * HD], F32R)
        wo_hi = place("wo_hi", [128, HP, D], F32R)
        wo_lo = place("wo_lo", [128, HP, D], F32R)
        embW = place("embW", [2 * PR, HPX, D])
        pix = place("pix", [2 * PR, GB, NPS, IMG])
        emb = place("emb", [2 * NP, 2, D])
        base = place("base", [T, D])
        hraw = place("hraw", [T, GB, D])
        xn = place("xn", [T, GB, D])
        hx = place("hx", [T, GB, D])
        h2 = place("h2", [T, GB, D])
        xT_hi = place("xT_hi", [128, KC, GT], F32R)
        xT_lo = place("xT_lo", [128, KC, GT], F32R)
        qT = place("qT", [128, 2, GT])
        kT = place("kT", [128, 2, GB, 2, T])
        vv = place("vv", [T, GB, HD])
        sm = place("sm", [T, 2, 4, T])
        pr = place("pr", [T, 4, 4, T])
        pT = place("pT", [T, 2, 4, T])
        oT_at = used[0]
        oT_hi = place("oT_hi", [128, HP, GT], F32R)
        oT_lo = place("oT_lo", [128, HP, GT], F32R)
        oT_end = used[0]
        x2T = place("x2T", [128, KC, GT])
        rows = place("rows", [T, GB, ROW])
        mx = place("mx", [T, 2, 4])
        nb = place("nb", [T, 2, 4])
        rs = place("rs", [T, 4, 4])
        rc = place("rc", [T, 4, 4])
        st1 = place("st1", [T, GB, 6])
        mv1 = place("mv1", [T, GB, 2])
        ve1 = place("ve1", [T, GB])
        rstd1 = place("rstd1", [T, GB])
        st2 = place("st2", [T, GB, 6])
        mv2 = place("mv2", [T, GB, 2])
        ve2 = place("ve2", [T, GB])
        rstd2 = place("rstd2", [T, GB])
        lg = place("lg", [T, GB, E])
        lmax = place("lmax", [T, GB])
        ls = place("ls", [T, GB, E])
        ex = place("ex", [T, GB, E])
        es = place("es", [T, GB])
        er = place("er", [T, GB])
        gmax = place("gmax", [T, GB])
        eq = place("eq", [T, GB, E])
        te = place("te", [T, GB, E])
        g2 = place("g2", [T, GB, E])
        pick = place("pick", [T, TOPK, GB])
        oh = place("oh", [T, TOPK, GB, E])
        chosen = place("chosen", [T, GB, E], BF16)
        before = place("before", [T, GB + 1, E], BF16)
        po_ = place("po_", [T, TOPK, GB, E])
        ps_ = place("ps_", [T, TOPK, GB])
        sl0 = place("sl0", [T, TOPK, GB])
        over = place("over", [T, TOPK, GB])
        slot = place("slot", [T, TOPK, GB], I32)
        tokid = place("tokid", [T, GB])
        tokid_i = place("tokid_i", [T, GB], I32)
        attention_end = used[0]

        used[0] = oT_at
        tok_raw = place("tok_raw", [128, KC, CH * PX * PX])
        b1_raw = place("b1_raw", [E * MC, 128])
        fill = place("fill", [T, CT, ROW])
        brow = place("brow", [T, D])
        assert used[0] <= oT_end and attention_end <= nc.sbuf_usable_end

        used[0] = shared
        w1_hi = place("w1_hi", [128, KC, HID], F32R)
        w1_lo = place("w1_lo", [128, KC, HID], F32R)
        w2_hi = place("w2_hi", [128, MC, D], F32R)
        w2_lo = place("w2_lo", [128, MC, D], F32R)
        b2b = place("b2b", [T, E, D])
        hid_hi = place("hid_hi", [128, MC, CAP], F32R)
        hid_lo = place("hid_lo", [128, MC, CAP], F32R)
        gl = place("gl", [128, 4, SPLIT_N[0]])
        xs = place("xs", [T, CT, ROW])
        xsT_hi = place("xsT_hi", [128, KC, CAP], F32R)
        xsT_lo = place("xsT_lo", [128, KC, CAP], F32R)
        gate = place("gate", [T, CT])
        dest = place("dest", [T, CT], I32)
        ysum = place("ysum", [T, CT, D])
        yout = place("yout", [T, CT, D])
        assert used[0] <= nc.sbuf_usable_end, used[0]

        def psum(name):
            return ctx.enter_context(nc.psum_tensor(name, [128, 512], F32))

        bank = [psum(f"bank{i}") for i in range(3)]
        score_bank = [psum(f"score_bank{i}") for i in range(2)]
        pT_bank = psum("pT_bank")
        o_bank = [psum(f"o_bank{i}") for i in range(2)]

        ident_zero, ident_done = sem("ident_zero"), sem("ident_done")
        mask_zero, masks_done = sem("mask_zero"), sem("masks_done")
        upto_one, consts_done = sem("upto_one"), sem("consts_done")
        fill_done, base_zero, key_pad = sem("fill_done"), sem("base_zero"), sem("key_pad")
        tokW_in, b1_in, small_in = sem("tokW_in"), sem("b1_in"), sem("small_in")
        stage_a_in, stage_b_in = sem("stage_a_in"), sem("stage_b_in")
        stage_a_hi, stage_b_hi = sem("stage_a_hi"), sem("stage_b_hi")
        stage_a_lo, stage_b_lo = sem("stage_a_lo"), sem("stage_b_lo")
        pix_in, tokens_in = sem("pix_in"), sem("tokens_in")
        slots_cleared, out_set = sem("slots_cleared"), sem("out_set")
        filled = sem("filled")
        act_drained, dve_drained = sem("act_drained"), sem("dve_drained")
        x_hi = sem("x_hi")
        scores_done, max_done, bias_done = sem("scores_done"), sem("max_done"), sem("bias_done")
        exp_done, recip_done, normed = sem("exp_done"), sem("recip_done"), sem("normed")
        pT_done, pT_copied = sem("pT_done"), sem("pT_copied")
        o_done, o_hi, o_lo = sem("o_done"), sem("o_hi"), sem("o_lo")
        based, hx_done = sem("based"), sem("hx_done")
        stats1, moments1, vareps1, rstd1_done, xn_done = (sem(n) for n in ("stats1", "moments1", "vareps1", "rstd1_done", "xn_done"))
        stats2, moments2, vareps2, rstd2_done, xn2_done = (sem(n) for n in ("stats2", "moments2", "vareps2", "rstd2_done", "xn2_done"))
        routed, lexp_done = sem("routed"), sem("lexp_done")
        dispatched = sem("dispatched")
        waits_passed = sem("waits_passed")
        b2_in, slots_in, meta_done = sem("b2_in"), sem("slots_in"), sem("meta_done")
        w1_hi_done, w1_lo_done, w2_hi_done, w2_lo_done = (sem(n) for n in ("w1_hi_done", "w1_lo_done", "w2_hi_done", "w2_lo_done"))
        w1_in, w2_in = sem("w1_in"), sem("w2_in")
        e_filled, gelu_done, hid_hi_done, hid_done = (sem(n) for n in ("e_filled", "gelu_done", "hid_hi_done", "hid_done"))
        xs_hi, xs_done, y_done, gated, added = (sem(n) for n in ("xs_hi", "xs_done", "y_done", "gated", "added"))

        block = ctx.enter_context(nc.Block())

        START = ([("W", "a")] * 4 + [("B", "d"), ("E", "d")] + [("X", "ad")] * 2
                 + [("V", "a"), ("V", "d")] * GB + [("Q", "d"), ("K", "ad"), ("Q", "d")])

        AT_E, AT_Y, AT_L, AT_C = 1, 5, 6, 13

        LAST_QK = PAIRS - 3

        def next_qk(n):
            return "KQ"[n % 2], n // 2 + 1 + n % 2

        def body_jobs(first, last):
            jobs = []
            for n in range(PAIRS):
                if n < LAST_QK:
                    jobs.append(next_qk(n) + (("ad", "d")[n % 2],))
                if not last and n == AT_E:
                    jobs.append(("E", 0, "d"))
                if not first and n == AT_Y:
                    jobs += [("Y", 0, "a"), ("Y", 1, "d")]
                if not first and n == AT_L:
                    jobs.append(("L", 0, "d"))
                if not first and n == AT_C:
                    jobs.append(("C", 0, "d"))
            if not last:
                jobs += [("X", 0, "ad"), ("X", 1, "ad")]
                for b in range(GB):
                    jobs += [("V", 2 * b, "a"), ("V", 2 * b + 1, "d")]
            jobs += [("O", 0, "d"), ("O", 1, "d")]
            if not last:
                jobs += [("Q", 0, "d"), ("K", 0, "ad"), ("Q", 1, "d")]
            return jobs

        START_JOBS = []
        seen = {}
        for name, by in START:
            START_JOBS.append((name, seen.get(name, 0), by))
            seen[name] = seen.get(name, 0) + 1
        END_JOBS = [("Y", 0, "a"), ("Y", 1, "d"), ("L", 0, "d"), ("C", 0, "d")]
        FIRST, STEADY, LAST = body_jobs(True, False), body_jobs(False, False), body_jobs(False, True)

        def count(jobs, engine=None):
            return sum(1 for j in jobs if engine is None or engine in j[2])

        def before_body(g, engine=None):
            n = count(START_JOBS, engine)
            if isinstance(g, int) and g == 0:
                return n
            n += count(FIRST, engine)
            k = count(STEADY, engine)
            return (g * k) + (n - k)

        def sequence(g):
            if isinstance(g, int) and g == 0:
                return START_JOBS + FIRST, len(START_JOBS)
            own = LAST if isinstance(g, int) and g == G - 1 else STEADY
            prev = START_JOBS + FIRST + STEADY
            return prev + own, len(prev)

        class Jobs:

            def __init__(self, where):
                if isinstance(where, str) and where == "start":
                    self.seq, self.at, self.g = START_JOBS, 0, None
                elif isinstance(where, str):
                    self.seq = START_JOBS + FIRST + STEADY * (G - 2) + LAST + END_JOBS
                    self.at, self.g = len(self.seq) - len(END_JOBS), None
                else:
                    self.seq, self.at = sequence(where)
                    self.g = where

            def index(self, name, k):
                for i in range(self.at, len(self.seq)):
                    if self.seq[i][:2] == (name, k):
                        return i
                raise KeyError((name, k))

            def bank(self, name, k):
                return bank[self.index(name, k) % len(bank)]

            def total(self, i, engine=None):
                own = count(self.seq[self.at:i + 1], engine) if i >= self.at else -count(self.seq[i + 1:self.at], engine)
                if self.g is None:
                    return count(self.seq[:i + 1], engine)
                return before_body(self.g, engine) + own

            def last_before(self, name, k):
                return max(i for i in range(self.at) if self.seq[i][:2] == (name, k))

            def filled(self, name, k):
                return self.total(self.index(name, k))

            def emptied(self, i):
                sems = {"a": act_drained, "d": dve_drained}
                return [(sems[e], self.total(i, e)) for e in self.seq[i][2]]

            def drained(self, name, k):
                return self.emptied(self.index(name, k))

            def bank_free(self, name, k):
                i = self.index(name, k) - len(bank)
                return self.emptied(i) if i >= 0 else []

        NF, NX = 2 * MC, len(XJOBS)
        EJ = NF + NX + CT
        ebanks = bank + o_bank

        def ebank(j):
            return ebanks[j % EB]

        def e_count(e, j, last=False):
            return EJ * e + (NX + j + 1 - (NX if last and j >= NF + NX else 0))

        def pair(g, n):
            return g * PAIRS + n

        def wait_all(eng, waits):
            for s, v in waits:
                eng.wait_ge(s, v)

        def halves(out_ap, a, b, start, stop, pe):
            pe.matmul(out_ap, a[0], b[0], start=start, stop=False)
            pe.matmul(out_ap, a[0], b[1], start=False, stop=False)
            return pe.matmul(out_ap, a[1], b[0], start=False, stop=stop)

        def wait_apart(eng, *waits):
            for s, v in waits:
                eng.wait_ge(s, v)
            if not all(isinstance(v, int) for _, v in waits):
                eng.sem_inc(waits_passed, 1)

        def attention_over(eng):
            eng.wait_ge(dispatched, 16 * TOPK * B)
            eng.wait_ge(out_set, 16 * G)

        @block.sync
        def _(sp):
            def load_pixels(g):
                for q in range(2):
                    for c in range(CH):
                        w = IMG - q * HPX
                        p0 = 2 * PX * c + q
                        for b in range(GB):
                            src = x[bass.ds(GB * g + b, 1), c, :, q * HPX:IMG].rearrange("b (n r) w -> r (b n) w", r=PX)
                            sp.dma_start(pix[p0:p0 + 2 * PX - 1:2, b, :, 0:w], src).then_inc(pix_in, 16)

            def load_text(g):
                sp.dma_start(hraw[1 + NP:T, :, :], txt[bass.ts(g, GB)].rearrange("b t d -> t b d")).then_inc(tokens_in, 16)
                sp.dma_start(hraw[0:1, :, :], cls_token.broadcast_to([1, GB, D])).then_inc(tokens_in, 16)

            def place_patches():
                for b in range(GB):
                    p0 = (b % 2) * NP
                    sp.dma_start(hraw[1:1 + NP, b, :], emb[p0:p0 + NP, b // 2, :]).then_inc(tokens_in, 16)

            def set_out(g):
                sp.dma_start(out[bass.ts(g, GT), :].rearrange("(b t) d -> t b d", t=T), h2[:, :, :]).then_inc(out_set, 16)

            sp.dma_start(tok_raw[:, :, :], tokW.rearrange("(c p) f -> p c f", p=128)).then_inc(tokW_in, 16)
            load_pixels(0)
            load_text(0)
            sp.dma_start(b1_raw[:, :], b1.rearrange("e (m p) -> (e m) p", p=128)).then_inc(b1_in, 16)
            sp.dma_start(stage_b[:, :].rearrange("p (c n) -> p c n", c=KC), Wq.rearrange("(c p) n -> p c n", p=128)).then_inc(stage_b_in, 16)
            sp.wait_ge(fill_done, 2)
            for e in range(E):
                sp.dma_start(slots[e * CAP:(e + 1) * CAP, :].rearrange("(t p) r -> p t r", p=T), fill[:, :, :]).then_inc(slots_cleared, 16)
            sp.dma_start(out[B * T:B * T + CAP, :].rearrange("(t p) r -> p t r", p=T), fill[:, :, 0:D]).then_inc(slots_cleared, 16)
            jobs = Jobs("start")
            wait_all(sp, jobs.drained("E", 0))
            place_patches()
            sp.wait_ge(filled, jobs.filled("E", 0))
            load_pixels(1)
            sp.wait_ge(stage_b_lo, 1)
            sp.dma_start(stage_b[:, :].rearrange("p (c n) -> p c n", c=HP), Wo.rearrange("(c p) n -> p c n", p=128)).then_inc(stage_b_in, 16)

            def body(g, first=False, last=False):
                jobs = Jobs(g)
                if not last:
                    sp.wait_ge(hx_done, g + 1)
                    load_text(g + 1)
                if not first:
                    wait_all(sp, jobs.emptied(jobs.last_before("O", 1)))
                    set_out(g - 1)
                if not last:
                    wait_all(sp, jobs.drained("E", 0))
                    place_patches()
                if not last and not (isinstance(g, int) and g == G - 2):
                    sp.wait_ge(filled, jobs.filled("E", 0))
                    load_pixels(g + 2)

            body(0, first=True)
            with sp.Fori(1, G - 2) as g:
                body(g)
            body(G - 2)
            body(G - 1, last=True)
            jobs = Jobs(G - 1)
            wait_all(sp, jobs.drained("O", 1))
            set_out(G - 1)

            sp.wait_ge(stage_a_lo, 2)
            sp.wait_ge(stage_b_lo, 2)
            def load_w1(e):
                sp.dma_start(stage_a[:, :].rearrange("p (c n) -> p c n", c=KC), w1[bass.ds(e, 1)].rearrange("e (c p) n -> p (e c) n", p=128)).then_inc(w1_in, 16)

            def load_w2(e):
                sp.dma_start(stage_b[:, :].rearrange("p (c n) -> p c n", c=MC), w2[bass.ds(e, 1)].rearrange("e (c p) n -> p (e c) n", p=128)).then_inc(w2_in, 16)

            def load_slots(e):
                sp.dma_start(xs[:, :, :], slots[bass.ts(e, CAP), :].rearrange("(t p) r -> p t r", p=T)).then_inc(slots_in, 16)

            load_w1(0)
            load_w2(0)
            attention_over(sp)
            sp.dma_start(b2b[:, :, :], b2.rearrange("(o e) d -> o e d", o=1).broadcast_to([T, E, D])).then_inc(b2_in, 16)
            load_slots(0)
            sp.wait_ge(w1_lo_done, 4)
            load_w1(1)

            def expert(e, last=False):
                sp.wait_ge(meta_done, 2 * e + 2)
                if not last:
                    load_slots(e + 1)
                sp.wait_ge(w2_lo_done, 4 * e + 4)
                if not last:
                    load_w2(e + 1)
                if not last and not (isinstance(e, int) and e == E - 2):
                    sp.wait_ge(w1_lo_done, 4 * e + 8)
                    load_w1(e + 2)

            with sp.Fori(0, E - 2) as e:
                expert(e)
            expert(E - 2)
            expert(E - 1, last=True)
            sp.wait_ge(added, 16 * CT * E)

        @block.gpsimd
        def _(pool):
            def after(*waits):
                wait_apart(pool, *waits)

            pool.memset(ident[:, :], 0.0).then_inc(ident_zero, 1)
            pool.wait_ge(ident_zero, 1)
            pool.affine_select(out=ident[:, :], in_=ident[:, :], compare_op=ALU.not_equal, fill=1.0, base=0,
                               pattern=[[-1, 128]], channel_multiplier=1).then_inc(ident_done, 1)
            pool.memset(fill[:, :, :], 0.0).then_inc(fill_done, 1)
            pool.memset(base[:, :], 0.0).then_inc(base_zero, 1)
            pool.memset(brow[:, :], 0.0).then_inc(base_zero, 1)
            pool.wait_ge(fill_done, 1)
            pool.iota(fill[:, :, ID:ID + 1], pattern=[[T, CT], [1, 1]], base=B * T, channel_multiplier=1,
                      allow_small_or_imprecise_dtypes=True).then_inc(fill_done, 1)
            pool.memset(mask[:, :], 0.0).then_inc(mask_zero, 1)
            pool.memset(upto[:, :], 1.0).then_inc(mask_zero, 1)
            pool.memset(ones[:, :], 1.0).then_inc(consts_done, 1)
            pool.memset(neg_half[:, :], -0.5).then_inc(consts_done, 1)
            pool.memset(rows[:, :, :], 0.0).then_inc(consts_done, 1)
            pool.memset(before[:, 0, :], 0.0).then_inc(consts_done, 1)
            pool.wait_ge(mask_zero, 2)
            pool.affine_select(out=mask[:, :], in_=mask[:, :], compare_op=ALU.is_ge, fill=NEG, base=0,
                               pattern=[[-1, T]], channel_multiplier=1).then_inc(consts_done, 1)
            pool.affine_select(out=upto[:, :], in_=upto[:, :], compare_op=ALU.is_ge, fill=0.0, base=0,
                               pattern=[[1, T]], channel_multiplier=-1).then_inc(consts_done, 1)
            pool.iota(io8[:, :, :], pattern=[[0, GB], [1, E]], base=-E, channel_multiplier=0,
                      allow_small_or_imprecise_dtypes=True).then_inc(consts_done, 1)
            pool.iota(tokid[:, :], pattern=[[T, GB]], base=0, channel_multiplier=1,
                      allow_small_or_imprecise_dtypes=True).then_inc(consts_done, 1)
            pool.wait_ge(small_in, SMALL)
            pool.tensor_tensor(base[0:1 + NP, :], base[0:1 + NP, :], brow[0:1 + NP, :], ALU.add).then_inc(consts_done, 1)

            def add_base(g):
                after((tokens_in, TOKENS * (g + 1)), (consts_done, CONSTS))
                pool.tensor_tensor(hraw[:, :, :], hraw[:, :, :], base[:, None, :].broadcast_to([T, GB, D]), ALU.add).then_inc(based, 1)

            def rstd(k, moments, vareps, done, mv, ve, out_t):
                after((moments, k + 1))
                pool.tensor_scalar(ve[:, :], mv[:, :, 1], EPS, 1.0, ALU.add, ALU.mult).then_inc(vareps, 1)
                after((vareps, k + 1))
                pool.tensor_tensor(out_t[:, :], ve[:, :], neg_half[:, :], ALU.pow).then_inc(done, 1)

            def dispatch(k, i):
                after((routed, ROUTE_STEPS * (k + 1)), (slots_cleared, 16 * (E + 1)))
                b, j = divmod(i, TOPK)
                pool.indirect_dma_start(slots, bass.IndirectOffsetOnAxis(ap=slot[:, j, b:b + 1], axis=0),
                                        rows[:, b, :], None, bounds_check=E * CAP - 1, oob_is_err=False).then_inc(dispatched, 16)

            add_base(0)
            rstd(0, moments1, vareps1, rstd1_done, mv1, ve1, rstd1)

            def body(g, first=False, last=False):
                for n in range(PAIRS + 1):
                    if n == 0:
                        if first:
                            after((xn_done, GB))
                        else:
                            jobs = Jobs(g)
                            after((xn_done, GB * (g + 1)), *jobs.emptied(jobs.last_before("O", 1)))
                        pool.tensor_tensor(hx[:, :, :], hraw[:, :, :], xn[:, :, :], ALU.add).then_inc(hx_done, 1)
                    if n >= 1:
                        m = n - 1
                        after((recip_done, pair(g, n)))
                        for i in range(4):
                            p = pool.tensor_scalar(pr[:, m % 4, i, :], pr[:, m % 4, i, :], rc[:, m % 4, i:i + 1], 1.0, ALU.mult, ALU.mult)
                        p.then_inc(normed, 1)
                    if n == 3 and not first:
                        rstd(g - 1, moments2, vareps2, rstd2_done, mv2, ve2, rstd2)
                    if n == 5 and not last:
                        add_base(g + 1)
                    if n == 7 and not last:
                        rstd(g + 1, moments1, vareps1, rstd1_done, mv1, ve1, rstd1)
                    if n == PAIRS and not first:
                        for i in range(TOPK * GB):
                            dispatch(g - 1, i)

            body(0, first=True)
            with pool.Fori(1, G - 1) as g:
                body(g)
            body(G - 1, last=True)
            rstd(G - 1, moments2, vareps2, rstd2_done, mv2, ve2, rstd2)
            for i in range(TOPK * GB):
                dispatch(G - 1, i)

            def split_w2(e):
                after((w2_in, 16 * e + 16))
                if not (isinstance(e, int) and e == 0):
                    after((e_filled, e_count(e, -1)))
                for k in range(4):
                    c = slice(2 * k, 2 * k + 2)
                    stage = stage_b[:, :].rearrange("p (c n) -> p c n", c=MC)
                    pool.tensor_copy(w2_hi[:, c, :], stage[:, c, :]).then_inc(w2_hi_done, 1)
                    after((w2_hi_done, 4 * e + k + 1))
                    pool.tensor_tensor(w2_lo[:, c, :], stage[:, c, :], w2_hi[:, c, :].bitcast(F32), ALU.subtract).then_inc(w2_lo_done, 1)

            def add_results(e):
                for t in range(CT):
                    after((y_done, CT * e + t + 1))
                    if t == 0:
                        if isinstance(e, int) and e == 0:
                            after((slots_cleared, 16 * (E + 1)))
                        else:
                            after((added, 16 * CT * e))
                    pool.tensor_scalar(yout[:, t, :], ysum[:, t, :], gate[:, t:t + 1], 1.0, ALU.mult, ALU.mult).then_inc(gated, 1)
                    after((gated, CT * e + t + 1))
                    pool.indirect_dma_start(out, bass.IndirectOffsetOnAxis(ap=dest[:, t:t + 1], axis=0),
                                            yout[:, t, :], None, compute_op=ALU.add).then_inc(added, 16)

            attention_over(pool)
            split_w2(0)
            add_results(0)
            with pool.Fori(1, E) as e:
                split_w2(e)
                add_results(e)

        @block.scalar
        def _(act):
            act.dma_start(stage_a[:, :].rearrange("p (c n) -> p c n", c=KC), Wv.rearrange("(c p) n -> p c n", p=128)).then_inc(stage_a_in, 16)
            act.dma_start(router_sb[:, :, :], router_w.rearrange("(c p) e -> p c e", p=128)).then_inc(small_in, 16)
            act.dma_start(router_bb[:, :, :], router_b.rearrange("(o b e) -> o b e", o=1, b=1).broadcast_to([T, GB, E])).then_inc(small_in, 16)
            act.wait_ge(base_zero, 2)
            act.dma_start(base[0:1 + NP, :], pos_enc[0, :, :]).then_inc(small_in, 16)
            act.dma_start(brow[1:1 + NP, :], tok_b.rearrange("(o d) -> o d", o=1).broadcast_to([NP, D])).then_inc(small_in, 16)

            def drain(jobs, name, k, dst, src, **kw):
                act.wait_ge(filled, jobs.filled(name, k))
                act.activation(dst, src, ACT.Copy, **kw).then_inc(act_drained, 1)

            def drain_x(jobs, k):
                drain(jobs, "X", k, xT_hi[:, k, :], jobs.bank("X", k)[:, 0:GT])

            def drain_k(jobs, c):
                drain(jobs, "K", c, kT[0:DK, c % 2, :, 0, :], jobs.bank("K", c)[0:DK, 0:GT].rearrange("p (b t) -> p b t", b=GB))

            def drain_v(jobs, b):
                drain(jobs, "V", 2 * b, vv[:, b, 0:512], jobs.bank("V", 2 * b)[0:T, :])

            def drain_y(jobs):
                drain(jobs, "Y", 0, x2T[:, 0, :], jobs.bank("Y", 0)[:, 0:GT])

            jobs = Jobs("start")
            for k in range(4):
                drain(jobs, "W", k, embW[:, 2 * k:2 * k + 2, :], jobs.bank("W", k)[0:2 * PR, :].rearrange("p (j d) -> p j d", j=2))
            act.wait_ge(stage_a_in, 16)
            act.activation(wqkv_hi[:, :, 2 * HD:], stage_a[:, :].rearrange("p (c n) -> p c n", c=KC), ACT.Copy).then_inc(stage_a_hi, 1)
            act.wait_ge(stage_b_in, 16)
            act.activation(wqkv_hi[:, :, 0:HD], stage_b[:, :].rearrange("p (c n) -> p c n", c=KC), ACT.Copy).then_inc(stage_b_hi, 1)
            act.wait_ge(stage_a_lo, 1)
            act.dma_start(stage_a[:, :].rearrange("p (c n) -> p c n", c=KC), Wk.rearrange("(c p) n -> p c n", p=128)).then_inc(stage_a_in, 16)
            for k in range(KC):
                drain_x(jobs, k)
            for b in range(GB):
                drain_v(jobs, b)
            act.wait_ge(stage_a_in, 32)
            act.activation(wqkv_hi[:, :, HD:2 * HD], stage_a[:, :].rearrange("p (c n) -> p c n", c=KC), ACT.Copy).then_inc(stage_a_hi, 1)
            act.wait_ge(key_pad, 1)
            drain_k(jobs, 0)
            act.wait_ge(stage_b_in, 32)
            act.activation(wo_hi[:, :, :], stage_b[:, :].rearrange("p (c n) -> p c n", c=HP), ACT.Copy).then_inc(stage_b_hi, 1)

            def router_exp(k):
                act.wait_ge(routed, ROUTE_STEPS * k + ROUTE_PARTS[0])
                act.activation(ex[:, :, :], ls[:, :, :], ACT.Exp).then_inc(lexp_done, 1)

            def body(g, first=False, last=False):
                jobs = Jobs(g)
                for n in range(PAIRS + 3):
                    if 3 <= n:
                        m = n - 3
                        c, b = m // 2, 2 * (m % 2)
                        act.wait_ge(o_done, pair(g, m + 1))
                        act.activation(oT_hi[:, c, b * T:(b + 2) * T], o_bank[m % 2][:, 0:2 * T], ACT.Copy).then_inc(o_hi, 1)
                    if 2 <= n < PAIRS + 2:
                        m = n - 2
                        act.wait_ge(pT_done, pair(g, m + 1))
                        act.activation(pT[:, m % 2, :, :], pT_bank[0:T, 0:4 * T].rearrange("p (i q) -> p i q", i=4), ACT.Copy).then_inc(pT_copied, 1)
                    if 1 <= n <= LAST_QK and n % 2 == 1:
                        drain_k(jobs, n // 2 + 1)
                    if not first and n == AT_Y + 1:
                        drain_y(jobs)
                    if n < PAIRS:
                        act.wait_ge(bias_done, pair(g, n + 1))
                        if not (first and n < 4):
                            act.wait_ge(pT_done, pair(g, n - 3))
                        for i in range(4):
                            a = act.activation(pr[:, n % 4, i, :], sm[:, n % 2, i, :], ACT.Exp, bias=nb[:, n % 2, i:i + 1],
                                               scale=SCALE, accum_out=rs[:, n % 4, i:i + 1])
                        a.then_inc(exp_done, 1)
                    if not first and n == AT_L + 2:
                        router_exp(g - 1)
                    if not last and n == PAIRS:
                        for k in range(KC):
                            drain_x(jobs, k)
                    if not last and n > PAIRS:
                        for b in range(2):
                            drain_v(jobs, 2 * (n - PAIRS - 1) + b)
                if not last:
                    drain_k(jobs, 0)

            body(0, first=True)
            with act.Fori(1, G - 1) as g:
                body(g)
            body(G - 1, last=True)
            drain_y(Jobs("end"))
            router_exp(G - 1)

            def split_w1(k):
                c = slice(k % 2 * 512, k % 2 * 512 + 512)
                act.activation(w1_hi[:, k // 2, c], stage_a[:, :].rearrange("p (c n) -> p c n", c=KC)[:, k // 2, c], ACT.Copy).then_inc(w1_hi_done, 1)

            def drain_slots(e, first=False):
                for i, (k, (t0, nt)) in enumerate(XJOBS):
                    j = NF + i
                    act.wait_ge(e_filled, i + 1 if first else e_count(e - 1, j))
                    act.activation(xsT_hi[:, k, t0 * T:(t0 + nt) * T], ebank(j)[:, 0:nt * T], ACT.Copy).then_inc(xs_hi, 1)

            def first_layer(e, first=False):
                for j in range(NF):
                    m, i = divmod(j, 2)
                    waits = [(e_filled, e_count(e, j))]
                    if not (first and j < 4):
                        waits.append((hid_done, NF * e + (j - 3)))
                    wait_apart(act, *waits)
                    act.activation(gl[:, j % 4, 0:SPLIT_N[i]], ebank(j)[:, 0:SPLIT_N[i]], ACT.Gelu,
                                   bias=b1T[:, bass.ds(MC * e + m, 1)]).then_inc(gelu_done, 1)

            def next_w1(e):
                act.wait_ge(w1_in, 16 * (e + 2))
                for k in range(4):
                    split_w1(k)

            attention_over(act)
            act.wait_ge(w1_in, 16)
            for k in range(4):
                split_w1(k)
            drain_slots(0, first=True)

            def expert(e, first=False, last=False):
                first_layer(e, first)
                if not last:
                    drain_slots(e + 1)
                    next_w1(e)

            expert(0, first=True)
            with act.Fori(1, E - 1) as e:
                expert(e)
            expert(E - 1, last=True)

        @block.vector
        def _(dve):
            def split_low(lo, whole, hi, done):
                dve.tensor_tensor(lo, whole, hi.bitcast(F32), ALU.subtract).then_inc(done, 1)

            def drain(jobs, name, k, dst, src):
                dve.wait_ge(filled, jobs.filled(name, k))
                dve.tensor_copy(dst, src).then_inc(dve_drained, 1)

            def drain_x(jobs, k):
                dve.wait_ge(filled, jobs.filled("X", k))
                dve.wait_ge(act_drained, jobs.total(jobs.index("X", k), "a"))
                split_low(xT_lo[:, k, :], jobs.bank("X", k)[:, 0:GT], xT_hi[:, k, :], dve_drained)

            def drain_q(jobs, c):
                drain(jobs, "Q", c, qT[:, c % 2, :], jobs.bank("Q", c)[:, 0:GT])

            def drain_k(jobs, c):
                drain(jobs, "K", c, kT[DK:128, c % 2, :, 1, :], jobs.bank("K", c)[DK:128, 0:GT].rearrange("p (b t) -> p b t", b=GB))

            def drain_v(jobs, b):
                drain(jobs, "V", 2 * b + 1, vv[:, b, 512:1024], jobs.bank("V", 2 * b + 1)[0:T, :])

            def drain_o(jobs, g, k):
                dve.wait_ge(filled, jobs.filled("O", k))
                if not (isinstance(g, int) and g == 0):
                    dve.wait_ge(out_set, 16 * g)
                dve.tensor_tensor(h2[:, 2 * k:2 * k + 2, :], jobs.bank("O", k)[0:T, :].rearrange("p (b d) -> p b d", b=2),
                                  hx[:, 2 * k:2 * k + 2, :], ALU.add).then_inc(dve_drained, 1)

            def moments(k, src, st, mv, stats, done):
                for b in range(GB):
                    dve.bn_stats(st[:, b, :], src[:, b, :]).then_inc(stats, 1)
                wait_apart(dve, (stats, GB * k + GB))
                for b in range(GB):
                    i = dve.bn_aggr(mv[:, b, :], st[:, b, :])
                i.then_inc(done, 1)

            def normalise(b, dst, src, mv, rstd, done):
                dve.tensor_scalar(dst, src, mv[:, b, 0:1], rstd[:, b:b + 1], ALU.subtract, ALU.mult).then_inc(done, 1)

            def drain_e(jobs):
                drain(jobs, "E", 0, emb[:, :, :], jobs.bank("E", 0)[0:2 * NP, :].rearrange("p (k d) -> p k d", k=2))

            dve.memset(kT[:, :, :, :, :], 0.0).then_inc(key_pad, 1)
            jobs = Jobs("start")
            drain(jobs, "B", 0, b1T[:, :], jobs.bank("B", 0)[:, 0:E * MC])
            drain_e(jobs)
            dve.wait_ge(stage_a_hi, 1)
            split_low(wqkv_lo[:, :, 2 * HD:], stage_a[:, :].rearrange("p (c n) -> p c n", c=KC), wqkv_hi[:, :, 2 * HD:], stage_a_lo)
            dve.wait_ge(based, 1)
            moments(0, hraw, st1, mv1, stats1, moments1)
            dve.wait_ge(stage_b_hi, 1)
            split_low(wqkv_lo[:, :, 0:HD], stage_b[:, :].rearrange("p (c n) -> p c n", c=KC), wqkv_hi[:, :, 0:HD], stage_b_lo)
            dve.wait_ge(rstd1_done, 1)
            for b in range(GB):
                normalise(b, xn[:, b, :], hraw[:, b, :], mv1, rstd1, xn_done)
            for k in range(KC):
                drain_x(jobs, k)
            for b in range(GB):
                drain_v(jobs, b)
            dve.wait_ge(stage_a_hi, 2)
            split_low(wqkv_lo[:, :, HD:2 * HD], stage_a[:, :].rearrange("p (c n) -> p c n", c=KC), wqkv_hi[:, :, HD:2 * HD], stage_a_lo)
            drain_q(jobs, 0)
            dve.wait_ge(key_pad, 1)
            drain_k(jobs, 0)
            drain_q(jobs, 1)
            dve.wait_ge(stage_b_hi, 2)
            split_low(wo_lo[:, :, :], stage_b[:, :].rearrange("p (c n) -> p c n", c=HP), wo_hi[:, :, :], stage_b_lo)
            dve.wait_ge(consts_done, CONSTS)

            def over_experts(ap):
                return ap[:, :, None].broadcast_to([T, GB, E])

            def route(jobs, k, part):
                at = [ROUTE_STEPS * k + sum(ROUTE_PARTS[:part])]
                made = [0]

                def step(ins):
                    ins.then_inc(routed, 1)
                    made[0] += 1

                def latest():
                    dve.wait_ge(routed, at[0] + made[0])

                if part == 0:
                    dve.wait_ge(filled, jobs.filled("L", 0))
                    dve.tensor_tensor(lg[:, :, :], jobs.bank("L", 0)[0:T, 0:GB * E].rearrange("p (b e) -> p b e", e=E),
                                      router_bb[:, :, :], ALU.add).then_inc(dve_drained, 1)
                    dve.wait_ge(dve_drained, jobs.drained("L", 0)[0][1])
                    step(dve.tensor_reduce(lmax[:, :], lg[:, :, :], AX.X, ALU.max))
                    latest()
                    step(dve.tensor_tensor(ls[:, :, :], lg[:, :, :], over_experts(lmax), ALU.subtract))
                if part == 1:
                    dve.wait_ge(lexp_done, k + 1)
                    step(dve.tensor_reduce(es[:, :], ex[:, :, :], AX.X, ALU.add))
                    latest()
                    step(dve.reciprocal(er[:, :], es[:, :]))
                    latest()
                    step(dve.tensor_tensor(rows[:, :, GATE0:GATE0 + E], ex[:, :, :], over_experts(er), ALU.mult))
                    step(dve.tensor_copy(rows[:, :, ID:ID + 1].rearrange("p b o -> p (b o)"), tokid[:, :]))
                    latest()
                    step(dve.tensor_scalar(tokid[:, :], tokid[:, :], float(GT), None, ALU.add))
                if part in (2, 3):
                    i = part - 2
                    gates = rows[:, :, GATE0:GATE0 + E] if i == 0 else g2[:, :, :]
                    if i == 1:
                        step(dve.scalar_tensor_tensor(out=g2[:, :, :], in0=oh[:, 0], scalar=-2.0, in1=rows[:, :, GATE0:GATE0 + E],
                                                      op0=ALU.mult, op1=ALU.add))
                        latest()
                    step(dve.tensor_reduce(gmax[:, :], gates, AX.X, ALU.max))
                    latest()
                    step(dve.tensor_tensor(eq[:, :, :], gates, over_experts(gmax), ALU.is_equal))
                    latest()
                    step(dve.tensor_tensor(te[:, :, :], eq[:, :, :], io8[:, :, :], ALU.mult))
                    latest()
                    step(dve.tensor_reduce(pick[:, i, :], te[:, :, :], AX.X, ALU.min))
                    latest()
                    step(dve.tensor_tensor(oh[:, i], io8[:, :, :], over_experts(pick[:, i, :]), ALU.is_equal))
                    latest()
                if part == 4:
                    step(dve.tensor_tensor(chosen[:, :, :], oh[:, 0], oh[:, 1], ALU.add))
                    for b in range(GB):
                        latest()
                        step(dve.tensor_tensor(before[:, b + 1, :], before[:, b, :], chosen[:, b, :], ALU.add))
                if part == 5:
                    dve.wait_ge(filled, jobs.filled("C", 0))
                    step(dve.tensor_copy(before[:, 0, :], before[:, GB, :]))
                    dve.tensor_tensor(po_[:, :, :, :], oh[:, :, :, :], jobs.bank("C", 0)[0:T, 0:GB * E].rearrange("p (o b e) -> p o b e", o=1, e=E).broadcast_to([T, TOPK, GB, E]),
                                      ALU.mult).then_inc(dve_drained, 1)
                    dve.wait_ge(dve_drained, jobs.drained("C", 0)[0][1])
                    step(dve.tensor_reduce(ps_[:, :, :], po_[:, :, :, :], AX.X, ALU.add))
                    latest()
                    step(dve.scalar_tensor_tensor(out=sl0[:, :, :], in0=pick[:, :, :], scalar=float(CAP), in1=ps_[:, :, :],
                                                  op0=ALU.mult, op1=ALU.add))
                    step(dve.tensor_scalar(over[:, :, :], ps_[:, :, :], float(CAP), OUT_OF_RANGE, ALU.is_gt, ALU.mult))
                    latest()
                    step(dve.scalar_tensor_tensor(out=slot[:, :, :], in0=sl0[:, :, :], scalar=float(E * CAP - 1), in1=over[:, :, :],
                                                  op0=ALU.add, op1=ALU.add))
                assert made[0] == ROUTE_PARTS[part], (part, made)

            def second_norm(k, part):
                if part == 0:
                    moments(k, h2, st2, mv2, stats2, moments2)
                else:
                    dve.wait_ge(rstd2_done, k + 1)
                    for b in range(GB):
                        normalise(b, rows[:, b, 0:D], h2[:, b, :], mv2, rstd2, xn2_done)

            ROUTE_AT = {AT_L + 1: (0,), AT_L + 3: (1,), AT_L + 4: (2,), AT_L + 5: (3,), AT_L + 6: (4,), AT_C + 1: (5,)}

            def body(g, first=False, last=False):
                jobs = Jobs(g)
                for n in range(PAIRS + 3):
                    if n < PAIRS:
                        wait_apart(dve, (scores_done, pair(g, n + 1)))
                        for i in range(4):
                            m = dve.tensor_tensor_reduce(sm[:, n % 2, i, :], score_bank[n % 2][0:T, i * T:(i + 1) * T], mask[:, :],
                                                         1.0, NEG, ALU.add, ALU.max, mx[:, n % 2, i:i + 1])
                        m.then_inc(max_done, 1)
                        dve.wait_ge(max_done, pair(g, n + 1))
                        dve.tensor_scalar(nb[:, n % 2, :], mx[:, n % 2, :], -SCALE, None, ALU.mult).then_inc(bias_done, 1)
                    if 1 <= n <= PAIRS:
                        dve.wait_ge(exp_done, pair(g, n))
                        dve.reciprocal(rc[:, (n - 1) % 4, :], rs[:, (n - 1) % 4, :]).then_inc(recip_done, 1)
                    if 1 <= n <= LAST_QK:
                        name, c = next_qk(n - 1)
                        (drain_k if name == "K" else drain_q)(jobs, c)
                    if 3 <= n:
                        m = n - 3
                        c, b = m // 2, 2 * (m % 2)
                        dve.wait_ge(o_hi, pair(g, m + 1))
                        split_low(oT_lo[:, c, b * T:(b + 2) * T], o_bank[m % 2][:, 0:2 * T], oT_hi[:, c, b * T:(b + 2) * T], o_lo)
                    if not last:
                        if n == AT_E + 1:
                            drain_e(jobs)
                        if n == 6:
                            dve.wait_ge(based, g + 2)
                            moments(g + 1, hraw, st1, mv1, stats1, moments1)
                        if n == 11:
                            dve.wait_ge(rstd1_done, g + 2)
                            dve.wait_ge(hx_done, g + 1)
                            for b in range(GB):
                                normalise(b, xn[:, b, :], hraw[:, b, :], mv1, rstd1, xn_done)
                        if n == PAIRS:
                            for k in range(KC):
                                drain_x(jobs, k)
                        if n > PAIRS:
                            for b in range(2):
                                drain_v(jobs, 2 * (n - PAIRS - 1) + b)
                    if not first:
                        if n == 1:
                            second_norm(g - 1, 0)
                        if n == 4:
                            second_norm(g - 1, 1)
                        if n == AT_Y + 1:
                            drain(jobs, "Y", 1, x2T[:, 1, :], jobs.bank("Y", 1)[:, 0:GT])
                        for part in ROUTE_AT.get(n, ()):
                            route(jobs, g - 1, part)
                for k in range(2):
                    drain_o(jobs, g, k)
                if not last:
                    drain_q(jobs, 0)
                    drain_k(jobs, 0)
                    drain_q(jobs, 1)
                if not first:
                    wait_apart(dve, (dispatched, 16 * TOPK * GB * g))

            body(0, first=True)
            with dve.Fori(1, G - 1) as g:
                body(g)
            body(G - 1, last=True)
            jobs = Jobs("end")
            dve.wait_ge(dve_drained, jobs.total(jobs.at - 1, "d"))
            second_norm(G - 1, 0)
            second_norm(G - 1, 1)
            drain(jobs, "Y", 1, x2T[:, 1, :], jobs.bank("Y", 1)[:, 0:GT])
            for part in range(6):
                route(jobs, G - 1, part)

            def w1_low(e):
                for k in range(4):
                    c = slice(k % 2 * 512, k % 2 * 512 + 512)
                    dve.wait_ge(w1_hi_done, 4 * e + k + 1)
                    split_low(w1_lo[:, k // 2, c], stage_a[:, :].rearrange("p (c n) -> p c n", c=KC)[:, k // 2, c], w1_hi[:, k // 2, c], w1_lo_done)

            def drain_slots(e):
                for i, (k, (t0, nt)) in enumerate(XJOBS):
                    dve.wait_ge(xs_hi, NX * e + i + 1)
                    split_low(xsT_lo[:, k, t0 * T:(t0 + nt) * T], ebank(NF + i)[:, 0:nt * T],
                              xsT_hi[:, k, t0 * T:(t0 + nt) * T], xs_done)

            def first_layer(e, first=False):
                for j in range(NF):
                    m, i = divmod(j, 2)
                    s, w = SPLIT_N[0] * i, SPLIT_N[i]
                    if j == 6:
                        if not first:
                            wait_apart(dve, (added, 16 * CT * e))
                        dve.tensor_copy(gate[:, :], xs[:, :, bass.ds(GATE0 + e, 1)].rearrange("p t o -> p (t o)")).then_inc(meta_done, 1)
                        dve.tensor_copy(dest[:, :], xs[:, :, ID:ID + 1].rearrange("p t o -> p (t o)")).then_inc(meta_done, 1)
                    dve.wait_ge(gelu_done, NF * e + j + 1)
                    dve.tensor_copy(hid_hi[:, m, s:s + w], gl[:, j % 4, 0:w]).then_inc(hid_hi_done, 1)
                    dve.wait_ge(hid_hi_done, NF * e + j + 1)
                    split_low(hid_lo[:, m, s:s + w], gl[:, j % 4, 0:w], hid_hi[:, m, s:s + w], hid_done)

            def second_layer(e, last=False):
                for t in range(CT):
                    j = NF + NX + t
                    dve.wait_ge(e_filled, e_count(e, j, last))
                    dve.tensor_tensor(ysum[:, t, :], ebank(j)[0:T, 0:D],
                                      b2b[:, bass.ds(e, 1), :].rearrange("p o d -> p (o d)"), ALU.add).then_inc(y_done, 1)

            def expert(e, first=False, last=False):
                first_layer(e, first)
                if not last:
                    drain_slots(e + 1)
                    w1_low(e + 1)
                second_layer(e, last)

            attention_over(dve)
            w1_low(0)
            drain_slots(0)
            dve.wait_ge(b2_in, 16)
            dve.wait_ge(slots_in, 16)
            expert(0, first=True)
            with dve.Fori(1, E - 1) as e:
                expert(e)
            expert(E - 1, last=True)

        @block.tensor
        def _(pe):
            def claim(jobs, name, k):
                wait_all(pe, jobs.bank_free(name, k))
                return jobs.bank(name, k)

            def embed(jobs):
                dst = claim(jobs, "E", 0)
                for k in range(2):
                    tokens = pix[:, 2 * k:2 * k + 2, :, :].rearrange("p b n w -> p (b n w)").rearrange("p (t j) -> p t j", j=PX)
                    for j in range(HPX):
                        m = pe.matmul(dst[0:2 * NP, k * D:(k + 1) * D], tokens[:, :, j], embW[:, j, :], start=(j == 0), stop=(j == HPX - 1))
                m.then_inc(filled, 1)

            def transpose_tokens(jobs, name, src, k):
                dst = claim(jobs, name, k)
                for b in range(GB):
                    m = pe.transpose(dst[:, b * T:(b + 1) * T], src[:, b, k * 128:(k + 1) * 128], ident[0:T, 0:T])
                m.then_inc(filled, 1)

            def project(jobs, name, c):
                dst = claim(jobs, name, c)[:, 0:GT]
                col = (0 if name == "Q" else HD) + c * 128
                for k in range(KC):
                    m = halves(dst, (wqkv_hi[:, k, col:col + 128], wqkv_lo[:, k, col:col + 128]),
                               (xT_hi[:, k, :], xT_lo[:, k, :]), k == 0, k == KC - 1, pe)
                m.then_inc(filled, 1)

            def project_v(jobs, i):
                b, half = divmod(i, 2)
                dst = claim(jobs, "V", i)[0:T, :]
                col = 2 * HD + half * 512
                for k in range(KC):
                    m = halves(dst, (xT_hi[:, k, b * T:(b + 1) * T], xT_lo[:, k, b * T:(b + 1) * T]),
                               (wqkv_hi[:, k, col:col + 512], wqkv_lo[:, k, col:col + 512]), k == 0, k == KC - 1, pe)
                m.then_inc(filled, 1)

            def project_o(jobs, i):
                dst = claim(jobs, "O", i)
                for b in (2 * i, 2 * i + 1):
                    for c in range(HP):
                        m = halves(dst[0:T, (b % 2) * D:(b % 2 + 1) * D],
                                   (oT_hi[:, c, b * T:(b + 1) * T], oT_lo[:, c, b * T:(b + 1) * T]),
                                   (wo_hi[:, c, :], wo_lo[:, c, :]), c == 0, c == HP - 1, pe)
                m.then_inc(filled, 1)

            jobs = Jobs("start")
            pe.wait_ge(ident_done, 1)
            pe.wait_ge(tokW_in, 16)
            for k in range(4):
                dst = claim(jobs, "W", k)
                for j in (2 * k, 2 * k + 1):
                    for dc in range(KC):
                        src = tok_raw[:, dc, :].rearrange("p (r j) -> p j r", j=HPX)[:, j]
                        o = (j % 2) * D + dc * 128
                        m = pe.transpose(dst[0:2 * PR, o:o + 128], src, ident[:, :])
                m.then_inc(filled, 1)
            pe.wait_ge(b1_in, 16)
            dst = claim(jobs, "B", 0)
            pe.transpose(dst[:, 0:E * MC], b1_raw[:, :], ident[0:E * MC, 0:E * MC]).then_inc(filled, 1)
            wait_all(pe, jobs.drained("W", 3))
            pe.wait_ge(pix_in, PIX)
            embed(jobs)
            for k in range(KC):
                pe.wait_ge(xn_done, GB)
                transpose_tokens(jobs, "X", xn, k)
            pe.wait_ge(stage_a_lo, 1)
            wait_all(pe, jobs.drained("X", 1))
            for i in range(2 * GB):
                project_v(jobs, i)
            pe.wait_ge(stage_b_lo, 1)
            project(jobs, "Q", 0)
            pe.wait_ge(stage_a_lo, 2)
            project(jobs, "K", 0)
            project(jobs, "Q", 1)
            pe.wait_ge(stage_b_lo, 2)
            pe.wait_ge(consts_done, CONSTS)
            pe.wait_ge(small_in, SMALL)
            pe.wait_ge(key_pad, 1)

            def scores(g, n, jobs, first):
                c, b0 = n // 2, 2 * (n % 2)
                if b0 == 0:
                    for name in ("Q", "K"):
                        early = c == 0 or (name, c) == ("Q", 1)
                        wait_all(pe, jobs.emptied(jobs.last_before(name, c) if early else jobs.index(name, c)))
                if not (first and n < 2):
                    pe.wait_ge(max_done, pair(g, n - 1))
                for b in range(2):
                    m = pe.matmul(score_bank[n % 2][0:T, b * 2 * T:(b + 1) * 2 * T], qT[:, c % 2, (b0 + b) * T:(b0 + b + 1) * T],
                                  kT[:, c % 2, b0 + b, :, :], start=True, stop=True)
                m.then_inc(scores_done, 1)

            def transpose_probs(g, n, first):
                pe.wait_ge(normed, pair(g, n + 1))
                if not (first and n < 1):
                    pe.wait_ge(pT_copied, pair(g, n))
                for i in range(4):
                    m = pe.transpose(pT_bank[0:T, i * T:(i + 1) * T], pr[:, n % 4, i, :], ident[0:T, 0:T])
                m.then_inc(pT_done, 1)

            def weigh_values(g, n, first):
                c, b0 = n // 2, 2 * (n % 2)
                pe.wait_ge(pT_copied, pair(g, n + 1))
                if not (first and n < 2):
                    pe.wait_ge(o_lo, pair(g, n - 1))
                for b in range(2):
                    for h in range(2):
                        v0 = (2 * c + h) * DK
                        m = pe.matmul(o_bank[n % 2][h * DK:(h + 1) * DK, b * T:(b + 1) * T], vv[:, b0 + b, v0:v0 + DK], pT[:, n % 2, 2 * b + h, :],
                                      start=True, stop=True)
                m.then_inc(o_done, 1)

            def logits(jobs):
                wait_all(pe, jobs.drained("Y", 0) + jobs.drained("Y", 1))
                dst = claim(jobs, "L", 0)
                for b in range(GB):
                    for c in range(KC):
                        m = pe.matmul(dst[0:T, b * E:(b + 1) * E], x2T[:, c, b * T:(b + 1) * T], router_sb[:, c, :], start=(c == 0), stop=(c == KC - 1))
                m.then_inc(filled, 1)

            def count_places(jobs, k):
                pe.wait_ge(routed, ROUTE_STEPS * k + sum(ROUTE_PARTS[:5]))
                dst = claim(jobs, "C", 0)[0:T, 0:GB * E]
                pe.matmul(dst, upto[:, :], chosen[:, :, :], start=True, stop=False)
                pe.matmul(dst, ones[:, :], before[:, 0:GB, :], start=False, stop=True).then_inc(filled, 1)

            def body(g, first=False, last=False):
                jobs = Jobs(g)
                for k in (2 * GB - 2, 2 * GB - 1):
                    wait_all(pe, jobs.emptied(jobs.last_before("V", k)))
                for n in range(PAIRS + 3):
                    if n < PAIRS:
                        scores(g, n, jobs, first)
                    if 3 <= n:
                        weigh_values(g, n - 3, first)
                    if 2 <= n < PAIRS + 2:
                        transpose_probs(g, n - 2, first)
                    if n < LAST_QK:
                        project(jobs, *next_qk(n))
                    if not last:
                        if n == AT_E:
                            pe.wait_ge(pix_in, PIX * (g + 2))
                            embed(jobs)
                        if n == PAIRS:
                            pe.wait_ge(xn_done, GB * (g + 2))
                            for k in range(KC):
                                transpose_tokens(jobs, "X", xn, k)
                        if n == PAIRS + 1:
                            wait_all(pe, jobs.drained("X", 1))
                        if n > PAIRS:
                            for i in range(4):
                                project_v(jobs, 4 * (n - PAIRS - 1) + i)
                    if not first:
                        if n == AT_Y:
                            pe.wait_ge(xn2_done, GB * g)
                            for k in range(KC):
                                transpose_tokens(jobs, "Y", rows, k)
                        if n == AT_L:
                            logits(jobs)
                        if n == AT_C:
                            count_places(jobs, g - 1)
                pe.wait_ge(o_lo, pair(g, PAIRS))
                for k in range(2):
                    project_o(jobs, k)
                if not last:
                    project(jobs, "Q", 0)
                    project(jobs, "K", 0)
                    project(jobs, "Q", 1)

            body(0, first=True)
            with pe.Fori(1, G - 1) as g:
                body(g)
            body(G - 1, last=True)
            jobs = Jobs("end")
            pe.wait_ge(xn2_done, GB * G)
            for k in range(KC):
                transpose_tokens(jobs, "Y", rows, k)
            logits(jobs)
            count_places(jobs, G - 1)

            def wait_bank(e, j, first=False, last=False):
                i = j - EB
                if last and i >= NF:
                    i -= EB
                if i < 0 and first:
                    if i + EB > 0:
                        pe.wait_ge(xs_done, i + EB)
                elif i < 0:
                    pe.wait_ge(y_done, CT * e + (i + 1))
                elif i < NF:
                    pe.wait_ge(gelu_done, NF * e + i + 1)
                elif i < NF + NX:
                    pe.wait_ge(xs_done, NX * (e + 1) + (i - NF + 1))

            def transpose_slots(e, first=False):
                pe.wait_ge(slots_in, 16 * (e + 1))
                for i, (k, (t0, nt)) in enumerate(XJOBS):
                    if not first:
                        wait_bank(e - 1, NF + i)
                    for t in range(nt):
                        m = pe.transpose(ebank(NF + i)[:, t * T:(t + 1) * T], xs[:, t0 + t, k * 128:(k + 1) * 128], ident[0:T, 0:T])
                    m.then_inc(e_filled, 1)

            def first_layer(e, first=False):
                pe.wait_ge(xs_done, NX * (e + 1))
                pe.wait_ge(w1_lo_done, 4 * (e + 1))
                for j in range(NF):
                    m_, i = divmod(j, 2)
                    wait_bank(e, j, first)
                    s, w = SPLIT_N[0] * i, SPLIT_N[i]
                    for k in range(KC):
                        m = halves(ebank(j)[:, 0:w], (w1_hi[:, k, m_ * 128:(m_ + 1) * 128], w1_lo[:, k, m_ * 128:(m_ + 1) * 128]),
                                   (xsT_hi[:, k, s:s + w], xsT_lo[:, k, s:s + w]), k == 0, k == KC - 1, pe)
                    m.then_inc(e_filled, 1)

            def second_layer(e, last=False):
                pe.wait_ge(hid_done, NF * (e + 1))
                pe.wait_ge(w2_lo_done, 4 * (e + 1))
                for t in range(CT):
                    j = NF + NX + t
                    wait_bank(e, j, last=last)
                    for m_ in range(MC):
                        m = halves(ebank(j)[0:T, 0:D], (hid_hi[:, m_, t * T:(t + 1) * T], hid_lo[:, m_, t * T:(t + 1) * T]),
                                   (w2_hi[:, m_, :], w2_lo[:, m_, :]), m_ == 0, m_ == MC - 1, pe)
                    m.then_inc(e_filled, 1)

            def expert(e, first=False, last=False):
                first_layer(e, first)
                if not last:
                    transpose_slots(e + 1)
                second_layer(e, last)

            transpose_slots(0, first=True)
            expert(0, first=True)
            with pe.Fori(1, E - 1) as e:
                expert(e)
            expert(E - 1, last=True)


_INS = ["x", "txt", "L0_tok_W", "L0_tok_b", "L0_tok_cls_token", "L0_tok_pos_enc", "L0_attn_Wq", "L0_attn_Wk",
        "L0_attn_Wv", "L0_attn_Wo", "L0_ffn_router_w", "L0_ffn_router_b", "L0_ffn_w1", "L0_ffn_b1", "L0_ffn_w2",
        "L0_ffn_b2"]


def kernel(**inputs):
    import numpy as np
    import concourse.bacc as bacc
    from concourse.bass_utils import run_bass_kernel_spmd

    nc = bacc.Bacc("TRN2", target_bir_lowering=False, num_devices=1)
    arrays, args = {}, []
    for name in _INS:
        a = np.ascontiguousarray(inputs[name])
        arrays[f"in_{name}_dram"] = a
        args.append(nc.dram_tensor(f"in_{name}_dram", a.shape, mybir.dt.from_np(a.dtype), kind="ExternalInput").ap())
    out = nc.dram_tensor("out_dram", (B * T + CAP, D), F32, kind="ExternalOutput").ap()
    slots = nc.dram_tensor("slots_dram", (E * CAP, ROW), F32).ap()
    build(nc, *args, out, slots)
    r = run_bass_kernel_spmd(nc, [arrays], core_ids=[0])
    return r.results[0]["out_dram"][0:B * T].reshape(B, T, D)
```

```python
from contextlib import ExitStack

import concourse.bass as bass
from concourse import mybir

F32 = mybir.dt.float32
F32R = mybir.dt.float32r
BF16 = mybir.dt.bfloat16
I32 = mybir.dt.int32
ALU = mybir.AluOpType
ACT = mybir.ActivationFunctionType
AX = mybir.AxisListType

B, CH, IMG = 32, 3, 96
PX = 16
NPS = IMG // PX
NP = NPS * NPS
TXT = 77
T = 1 + NP + TXT
D = 256
H, DK = 16, 64
HD = H * DK
E, HID = 8, 1024
TOPK = 2
CAP = -(-B * T * 5 // (4 * E))
EPS = 1e-5
SCALE = DK ** -0.5
NEG = -3.0e38
OUT_OF_RANGE = 16384.0

GB = 4
G = B // GB
GT = GB * T
KC = D // 128
HP = H // 2
PAIRS = HP * GB // 2
PR = CH * PX
HPX = PX // 2
ROW = 272
GATE0, ID = D, D + E
CT = CAP // T
MC = HID // 128
SPLIT_N = (288, CAP - 288)
FIRST_TILES = SPLIT_N[0] // T
SLOT_PARTS = ((0, 3), (3, CT - 3))
XJOBS = [(k, part) for part in SLOT_PARTS for k in range(KC)]
EB = 5
ROUTE_PARTS = (2, 5, 5, 6, 5, 5)
ROUTE_STEPS = sum(ROUTE_PARTS)
CONSTS, SMALL = 9, 64
PIX_ROWS = 16 * CH * GB // 2
TOKENS = 16 * 4
assert CAP == CT * T and GT <= 512 and IMG == NPS * PX


def build(nc, x, txt, tokW, tok_b, cls_token, pos_enc, Wq, Wk, Wv, Wo,
          router_w, router_b, w1, b1, w2, b2, out, slots):
    ctx = ExitStack()
    with ctx:
        def sem(name):
            return ctx.enter_context(nc.semaphore(name))

        base_addr = -(-nc.sbuf_base // 32) * 32
        used = [base_addr]

        def place(name, shape, dt=F32):
            size = 2 if dt == BF16 else 4
            for n in shape[1:]:
                size *= n
            t = nc.alloc_sbuf_tensor_at(name, shape, dt, offset=used[0])
            used[0] += -(-size // 32) * 32
            return t

        ident = place("ident", [128, 128])
        b1T = place("b1T", [128, E * MC])
        stage_a = place("stage_a", [128, 2048])
        stage_b = place("stage_b", [128, 2048])
        neg_half = place("neg_half", [T, GB])
        shared = used[0]

        mask = place("mask", [T, T])
        upto = place("upto", [T, T], BF16)
        ones = place("ones", [T, T], BF16)
        router_sb = place("router_sb", [128, KC, E])
        router_bb = place("router_bb", [T, GB, E])
        io8 = place("io8", [T, GB, E])
        wqkv_hi = place("wqkv_hi", [128, KC, 3 * HD], F32R)
        wqkv_lo = place("wqkv_lo", [128, KC, 3 * HD], F32R)
        wo_hi = place("wo_hi", [128, HP, D], F32R)
        wo_lo = place("wo_lo", [128, HP, D], F32R)
        embW = place("embW", [2 * PR, HPX, D])
        pix = place("pix", [2 * PR, GB, NPS, IMG])
        embT = place("embT", [128, KC, GB * NP])
        emb = place("emb", [2 * NP, 2, D])
        base = place("base", [T, D])
        hraw = place("hraw", [T, GB, D])
        xn = place("xn", [T, GB, D])
        hx = place("hx", [T, GB, D])
        h2 = place("h2", [T, GB, D])
        xT_hi = place("xT_hi", [128, KC, GT], F32R)
        xT_lo = place("xT_lo", [128, KC, GT], F32R)
        qT = place("qT", [128, 2, GT])
        kT = place("kT", [128, 2, GB, 2, T])
        vv = place("vv", [T, GB, HD])
        sm = place("sm", [T, 2, 4, T])
        pr = place("pr", [T, 4, 4, T])
        pT = place("pT", [T, 2, 4, T])
        oT_at = used[0]
        oT_hi = place("oT_hi", [128, HP, GT], F32R)
        oT_lo = place("oT_lo", [128, HP, GT], F32R)
        oT_end = used[0]
        x2T = place("x2T", [128, KC, GT])
        rows = place("rows", [T, GB, ROW])
        mx = place("mx", [T, 2, 4])
        nb = place("nb", [T, 2, 4])
        rs = place("rs", [T, 4, 4])
        rc = place("rc", [T, 4, 4])
        st1 = place("st1", [T, GB, 6])
        mv1 = place("mv1", [T, GB, 2])
        ve1 = place("ve1", [T, GB])
        rstd1 = place("rstd1", [T, GB])
        st2 = place("st2", [T, GB, 6])
        mv2 = place("mv2", [T, GB, 2])
        ve2 = place("ve2", [T, GB])
        rstd2 = place("rstd2", [T, GB])
        lg = place("lg", [T, GB, E])
        lmax = place("lmax", [T, GB])
        ls = place("ls", [T, GB, E])
        ex = place("ex", [T, GB, E])
        es = place("es", [T, GB])
        er = place("er", [T, GB])
        gmax = place("gmax", [T, GB])
        eq = place("eq", [T, GB, E])
        te = place("te", [T, GB, E])
        g2 = place("g2", [T, GB, E])
        pick = place("pick", [T, TOPK, GB])
        oh = place("oh", [T, TOPK, GB, E])
        chosen = place("chosen", [T, GB, E], BF16)
        before = place("before", [T, GB + 1, E], BF16)
        po_ = place("po_", [T, TOPK, GB, E])
        ps_ = place("ps_", [T, TOPK, GB])
        sl0 = place("sl0", [T, TOPK, GB])
        over = place("over", [T, TOPK, GB])
        slot = place("slot", [T, TOPK, GB], I32)
        tokid = place("tokid", [T, GB])
        tokid_i = place("tokid_i", [T, GB], I32)
        attention_end = used[0]

        used[0] = oT_at
        tok_raw = place("tok_raw", [128, KC, CH * PX * PX])
        b1_raw = place("b1_raw", [E * MC, 128])
        fill = place("fill", [T, CT, ROW])
        brow = place("brow", [T, D])
        assert used[0] <= oT_end and attention_end <= nc.sbuf_usable_end

        used[0] = shared
        w1_hi = place("w1_hi", [128, KC, HID], F32R)
        w1_lo = place("w1_lo", [128, KC, HID], F32R)
        w2_hi = place("w2_hi", [128, MC, D], F32R)
        w2_lo = place("w2_lo", [128, MC, D], F32R)
        b2b = place("b2b", [T, E, D])
        hid_hi = place("hid_hi", [128, MC, CAP], F32R)
        hid_lo = place("hid_lo", [128, MC, CAP], F32R)
        gl = place("gl", [128, 4, SPLIT_N[0]])
        xs = place("xs", [T, CT, ROW])
        xsT_hi = place("xsT_hi", [128, KC, CAP], F32R)
        xsT_lo = place("xsT_lo", [128, KC, CAP], F32R)
        gate = place("gate", [T, CT])
        dest = place("dest", [T, CT], I32)
        ysum = place("ysum", [T, CT, D])
        yout = place("yout", [T, CT, D])
        assert used[0] <= nc.sbuf_usable_end, used[0]

        def psum(name):
            return ctx.enter_context(nc.psum_tensor(name, [128, 512], F32))

        bank = [psum(f"bank{i}") for i in range(3)]
        score_bank = [psum(f"score_bank{i}") for i in range(2)]
        pT_bank = psum("pT_bank")
        o_bank = [psum(f"o_bank{i}") for i in range(2)]

        ident_zero, ident_done = sem("ident_zero"), sem("ident_done")
        mask_zero, consts_done = sem("mask_zero"), sem("consts_done")
        fill_done, base_zero, key_pad = sem("fill_done"), sem("base_zero"), sem("key_pad")
        tokW_in, b1_in, small_in = sem("tokW_in"), sem("b1_in"), sem("small_in")
        stage_a_in, stage_b_in = sem("stage_a_in"), sem("stage_b_in")
        stage_a_hi, stage_b_hi = sem("stage_a_hi"), sem("stage_b_hi")
        stage_a_lo, stage_b_lo = sem("stage_a_lo"), sem("stage_b_lo")
        rows_in = [sem(f"rows_in{i}") for i in range(2)]
        pix_in, tokens_in = sem("pix_in"), sem("tokens_in")
        embedded, embT_done = sem("embedded"), sem("embT_done")
        slots_cleared, out_set = sem("slots_cleared"), sem("out_set")
        filled = sem("filled")
        act_drained, dve_drained = sem("act_drained"), sem("dve_drained")
        scores_done, max_done, bias_done = sem("scores_done"), sem("max_done"), sem("bias_done")
        exp_done, recip_done, normed = sem("exp_done"), sem("recip_done"), sem("normed")
        pT_done, pT_copied = sem("pT_done"), sem("pT_copied")
        o_done, o_hi, o_lo = sem("o_done"), sem("o_hi"), sem("o_lo")
        based, first_based, hx_done = sem("based"), sem("first_based"), sem("hx_done")
        stats1, moments1, vareps1, rstd1_done, xn_done = (sem(n) for n in ("stats1", "moments1", "vareps1", "rstd1_done", "xn_done"))
        stats2, moments2, vareps2, rstd2_done, xn2_done = (sem(n) for n in ("stats2", "moments2", "vareps2", "rstd2_done", "xn2_done"))
        routed, lexp_done = sem("routed"), sem("lexp_done")
        dispatched = sem("dispatched")
        waits_passed = sem("waits_passed")
        b2_in, slots_in, meta_done = sem("b2_in"), sem("slots_in"), sem("meta_done")
        w1_hi_done, w1_lo_done, w2_hi_done, w2_lo_done = (sem(n) for n in ("w1_hi_done", "w1_lo_done", "w2_hi_done", "w2_lo_done"))
        w1_in, w2_in = sem("w1_in"), sem("w2_in")
        e_filled, gelu_done, hid_hi_done, hid_done = (sem(n) for n in ("e_filled", "gelu_done", "hid_hi_done", "hid_done"))
        xs_hi, xs_done, y_done, gated, added = (sem(n) for n in ("xs_hi", "xs_done", "y_done", "gated", "added"))

        block = ctx.enter_context(nc.Block())

        START = ([("W", "a")] * 4 + [("B", "d"), ("E", "d")] + [("X", "ad")] * 2
                 + [("V", "a"), ("V", "d")] * GB + [("Q", "d"), ("K", "ad"), ("Q", "d")])

        AT_E, AT_Y, AT_L, AT_X = 1, 8, 12, 13
        V_FIRST = {AT_X + 1: (0,), AT_X + 2: (1, 2), AT_X + 3: (3,)}
        V_SECOND = {PAIRS + 1: (0, 1), PAIRS + 2: (2, 3)}
        STATS2, MOMENTS2, NORM2 = {1: (0, 1), 2: (2, 3)}, 3, {5: (0, 1), 6: (2, 3)}
        STATS1, MOMENTS1, NORM1 = {7: (0, 1), 8: (2, 3)}, 8, {10: (0, 1), 11: (2, 3)}
        AT_BASE, AT_RSTD1, AT_RSTD2 = 5, 9, 4
        WO_AT, WO_PARTS = 4, 4
        ROUTE_AT = {AT_L + 3: 1, PAIRS: 2, PAIRS + 1: 3, PAIRS + 2: 4}

        LAST_QK = PAIRS - 3

        def next_qk(n):
            return "KQ"[n % 2], n // 2 + 1 + n % 2

        def body_jobs(first, last):
            jobs = []
            for n in range(PAIRS + 3):
                if n < LAST_QK:
                    jobs.append(next_qk(n) + (("ad", "d")[n % 2],))
                if not last and n == AT_E:
                    jobs.append(("E", 0, "d"))
                if not first and n == AT_Y:
                    jobs += [("Y", 0, "a"), ("Y", 1, "d")]
                if not first and n == AT_L:
                    jobs.append(("L", 0, "d"))
                if not last and n == AT_X:
                    jobs += [("X", 0, "ad"), ("X", 1, "ad")]
                if not last:
                    jobs += [("V", 2 * b, "a") for b in V_FIRST.get(n, ())]
                    jobs += [("V", 2 * b + 1, "d") for b in V_SECOND.get(n, ())]
            if not first:
                jobs.append(("C", 0, "d"))
            jobs += [("O", 0, "d"), ("O", 1, "d")]
            if not last:
                jobs += [("Q", 0, "d"), ("K", 0, "ad"), ("Q", 1, "d")]
            return jobs

        START_JOBS = []
        seen = {}
        for name, by in START:
            START_JOBS.append((name, seen.get(name, 0), by))
            seen[name] = seen.get(name, 0) + 1
        END_JOBS = [("Y", 0, "a"), ("Y", 1, "d"), ("L", 0, "d"), ("C", 0, "d")]
        FIRST, STEADY, LAST = body_jobs(True, False), body_jobs(False, False), body_jobs(False, True)

        def count(jobs, engine=None):
            return sum(1 for j in jobs if engine is None or engine in j[2])

        def before_body(g, engine=None):
            n = count(START_JOBS, engine)
            if isinstance(g, int) and g == 0:
                return n
            n += count(FIRST, engine)
            k = count(STEADY, engine)
            return (g * k) + (n - k)

        def sequence(g):
            if isinstance(g, int) and g == 0:
                return START_JOBS + FIRST, len(START_JOBS)
            own = LAST if isinstance(g, int) and g == G - 1 else STEADY
            prev = START_JOBS + FIRST + STEADY
            return prev + own, len(prev)

        class Jobs:

            def __init__(self, where):
                if isinstance(where, str) and where == "start":
                    self.seq, self.at, self.g = START_JOBS, 0, None
                elif isinstance(where, str):
                    self.seq = START_JOBS + FIRST + STEADY * (G - 2) + LAST + END_JOBS
                    self.at, self.g = len(self.seq) - len(END_JOBS), None
                else:
                    self.seq, self.at = sequence(where)
                    self.g = where

            def index(self, name, k):
                for i in range(self.at, len(self.seq)):
                    if self.seq[i][:2] == (name, k):
                        return i
                raise KeyError((name, k))

            def bank(self, name, k):
                return bank[self.index(name, k) % len(bank)]

            def total(self, i, engine=None):
                own = count(self.seq[self.at:i + 1], engine) if i >= self.at else -count(self.seq[i + 1:self.at], engine)
                if self.g is None:
                    return count(self.seq[:i + 1], engine)
                return before_body(self.g, engine) + own

            def last_before(self, name, k):
                return max(i for i in range(self.at) if self.seq[i][:2] == (name, k))

            def filled(self, name, k):
                return self.total(self.index(name, k))

            def emptied(self, i):
                sems = {"a": act_drained, "d": dve_drained}
                return [(sems[e], self.total(i, e)) for e in self.seq[i][2]]

            def drained(self, name, k):
                return self.emptied(self.index(name, k))

            def bank_free(self, name, k):
                i = self.index(name, k) - len(bank)
                return self.emptied(i) if i >= 0 else []

        NF, NX = 2 * MC, len(XJOBS)
        EJ = NF + NX + CT
        ebanks = bank + o_bank

        def ebank(j):
            return ebanks[j % EB]

        def e_count(e, j, last=False):
            return EJ * e + (NX + j + 1 - (NX if last and j >= NF + NX else 0))

        def pair(g, n):
            return g * PAIRS + n

        def wait_all(eng, waits):
            for s, v in waits:
                eng.wait_ge(s, v)

        def halves(out_ap, a, b, start, stop, pe):
            pe.matmul(out_ap, a[0], b[0], start=start, stop=False)
            pe.matmul(out_ap, a[0], b[1], start=False, stop=False)
            return pe.matmul(out_ap, a[1], b[0], start=False, stop=stop)

        def wait_apart(eng, *waits):
            for s, v in waits:
                eng.wait_ge(s, v)
            if not all(isinstance(v, int) for _, v in waits):
                eng.sem_inc(waits_passed, 1)

        def attention_over(eng):
            eng.wait_ge(dispatched, 16 * TOPK * B)
            eng.wait_ge(out_set, 16 * G)

        @block.sync
        def _(sp):
            def load_pixels(g):
                for b in range(GB):
                    for c in range(CH):
                        src = x[bass.ds(GB * g + b, 1), c].rearrange("b (n r) w -> r (b n) w", r=PX)
                        sp.dma_start(pix[2 * PX * c:2 * PX * (c + 1):2, b, :, :], src).then_inc(rows_in[b // 2], 16)
                flat = pix[:, :, :, :].rearrange("p b n w -> p (b n w)")
                half = GB // 2 * NPS * IMG
                for i in range(2):
                    sp.wait_ge(rows_in[i], PIX_ROWS * (g + 1))
                    end = (i + 1) * half - HPX
                    start = 0 if i == 0 else half - HPX
                    sp.dma_start(flat[1:2 * PR:2, start:end], flat[0:2 * PR:2, start + HPX:end + HPX]).then_inc(pix_in, 16)

            def load_text(g):
                sp.dma_start(hraw[1 + NP:T, :, :], txt[bass.ts(g, GB)].rearrange("b t d -> t b d")).then_inc(tokens_in, 16)
                sp.dma_start(hraw[0:1, :, :], cls_token.broadcast_to([1, GB, D])).then_inc(tokens_in, 16)

            def place_patches():
                for q in range(2):
                    sp.dma_start(hraw[1:1 + NP, q:GB:2, :], emb[q * NP:(q + 1) * NP, :, :]).then_inc(tokens_in, 16)

            def set_out(g):
                sp.dma_start(out[bass.ts(g, GT), :].rearrange("(b t) d -> t b d", t=T), h2[:, :, :]).then_inc(out_set, 16)

            sp.dma_start(tok_raw[:, :, :], tokW.rearrange("(c p) f -> p c f", p=128)).then_inc(tokW_in, 16)
            load_pixels(0)
            load_text(0)
            sp.dma_start(stage_b[:, :].rearrange("p (c n) -> p c n", c=KC), Wq.rearrange("(c p) n -> p c n", p=128)).then_inc(stage_b_in, 16)
            jobs = Jobs("start")
            wait_all(sp, jobs.drained("E", 0))
            place_patches()
            load_pixels(1)
            sp.wait_ge(fill_done, 2)
            for e in range(E):
                sp.dma_start(slots[e * CAP:(e + 1) * CAP, :].rearrange("(t p) r -> p t r", p=T), fill[:, :, :]).then_inc(slots_cleared, 16)
            sp.dma_start(out[B * T:B * T + CAP, :].rearrange("(t p) r -> p t r", p=T), fill[:, :, 0:D]).then_inc(slots_cleared, 16)
            sp.wait_ge(stage_b_lo, 1)
            sp.dma_start(stage_b[:, :].rearrange("p (c n) -> p c n", c=HP), Wo.rearrange("(c p) n -> p c n", p=128)).then_inc(stage_b_in, 16)

            def body(g, first=False, last=False):
                jobs = Jobs(g)
                if not last and not (isinstance(g, int) and g == G - 2):
                    sp.wait_ge(embedded, g + 2)
                    load_pixels(g + 2)
                if not last:
                    sp.wait_ge(hx_done, 2 * g + 2)
                    load_text(g + 1)
                if not first:
                    wait_all(sp, jobs.emptied(jobs.last_before("O", 1)))
                    set_out(g - 1)
                if not last:
                    wait_all(sp, jobs.drained("E", 0))
                    place_patches()

            body(0, first=True)
            with sp.Fori(1, G - 2) as g:
                body(g)
            body(G - 2)
            body(G - 1, last=True)
            jobs = Jobs(G - 1)
            wait_all(sp, jobs.drained("O", 1))
            set_out(G - 1)

            sp.wait_ge(stage_a_lo, 2)
            sp.wait_ge(stage_b_lo, 1 + WO_PARTS)
            def load_w1(e):
                sp.dma_start(stage_a[:, :].rearrange("p (c n) -> p c n", c=KC), w1[bass.ds(e, 1)].rearrange("e (c p) n -> p (e c) n", p=128)).then_inc(w1_in, 16)

            def load_w2(e):
                sp.dma_start(stage_b[:, :].rearrange("p (c n) -> p c n", c=MC), w2[bass.ds(e, 1)].rearrange("e (c p) n -> p (e c) n", p=128)).then_inc(w2_in, 16)

            def load_slots(e):
                sp.dma_start(xs[:, :, :], slots[bass.ts(e, CAP), :].rearrange("(t p) r -> p t r", p=T)).then_inc(slots_in, 16)

            load_w1(0)
            load_w2(0)
            attention_over(sp)
            load_slots(0)
            sp.dma_start(b2b[:, :, :], b2.rearrange("(o e) d -> o e d", o=1).broadcast_to([T, E, D])).then_inc(b2_in, 16)
            sp.wait_ge(w1_lo_done, 4)
            load_w1(1)

            def expert(e, last=False):
                sp.wait_ge(meta_done, 2 * e + 2)
                if not last:
                    load_slots(e + 1)
                sp.wait_ge(w2_lo_done, 4 * e + 4)
                if not last:
                    load_w2(e + 1)
                if not last and not (isinstance(e, int) and e == E - 2):
                    sp.wait_ge(w1_lo_done, 4 * e + 8)
                    load_w1(e + 2)

            with sp.Fori(0, E - 2) as e:
                expert(e)
            expert(E - 2)
            expert(E - 1, last=True)
            sp.wait_ge(added, 16 * CT * E)

        @block.gpsimd
        def _(pool):
            def after(*waits):
                wait_apart(pool, *waits)

            pool.memset(ident[:, :], 0.0).then_inc(ident_zero, 1)
            pool.wait_ge(ident_zero, 1)
            pool.affine_select(out=ident[:, :], in_=ident[:, :], compare_op=ALU.not_equal, fill=1.0, base=0,
                               pattern=[[-1, 128]], channel_multiplier=1).then_inc(ident_done, 1)
            pool.memset(fill[:, :, :], 0.0).then_inc(fill_done, 1)
            pool.memset(base[:, :], 0.0).then_inc(base_zero, 1)
            pool.memset(brow[:, :], 0.0).then_inc(base_zero, 1)
            pool.wait_ge(fill_done, 1)
            pool.iota(fill[:, :, ID:ID + 1], pattern=[[T, CT], [1, 1]], base=B * T, channel_multiplier=1,
                      allow_small_or_imprecise_dtypes=True).then_inc(fill_done, 1)
            pool.memset(mask[:, :], 0.0).then_inc(mask_zero, 1)
            pool.memset(upto[:, :], 1.0).then_inc(mask_zero, 1)
            pool.memset(ones[:, :], 1.0).then_inc(consts_done, 1)
            pool.memset(neg_half[:, :], -0.5).then_inc(consts_done, 1)
            pool.memset(rows[:, :, :], 0.0).then_inc(consts_done, 1)
            pool.memset(before[:, 0, :], 0.0).then_inc(consts_done, 1)
            pool.wait_ge(mask_zero, 2)
            pool.affine_select(out=mask[:, :], in_=mask[:, :], compare_op=ALU.is_ge, fill=NEG, base=0,
                               pattern=[[-1, T]], channel_multiplier=1).then_inc(consts_done, 1)
            pool.affine_select(out=upto[:, :], in_=upto[:, :], compare_op=ALU.is_ge, fill=0.0, base=0,
                               pattern=[[1, T]], channel_multiplier=-1).then_inc(consts_done, 1)
            pool.iota(io8[:, :, :], pattern=[[0, GB], [1, E]], base=-E, channel_multiplier=0,
                      allow_small_or_imprecise_dtypes=True).then_inc(consts_done, 1)
            pool.iota(tokid[:, :], pattern=[[T, GB]], base=0, channel_multiplier=1,
                      allow_small_or_imprecise_dtypes=True).then_inc(consts_done, 1)
            pool.wait_ge(small_in, SMALL)
            pool.tensor_tensor(base[0:1 + NP, :], base[0:1 + NP, :], brow[0:1 + NP, :], ALU.add).then_inc(consts_done, 1)

            def add_base(g, half):
                if half == 0:
                    after((tokens_in, TOKENS * (g + 1)), (consts_done, CONSTS))
                b = slice(2 * half, 2 * half + 2)
                pool.tensor_tensor(hraw[:, b, :], hraw[:, b, :], base[:, None, :].broadcast_to([T, 2, D]), ALU.add).then_inc(based, 1)

            def rstd(k, moments, vareps, done, mv, ve, out_t):
                after((moments, k + 1))
                pool.tensor_scalar(ve[:, :], mv[:, :, 1], EPS, 1.0, ALU.add, ALU.mult).then_inc(vareps, 1)
                after((vareps, k + 1))
                pool.tensor_tensor(out_t[:, :], ve[:, :], neg_half[:, :], ALU.pow).then_inc(done, 1)

            def dispatch(k, i):
                after((routed, ROUTE_STEPS * (k + 1)), (slots_cleared, 16 * (E + 1)))
                b, j = divmod(i, TOPK)
                pool.indirect_dma_start(slots, bass.IndirectOffsetOnAxis(ap=slot[:, j, b:b + 1], axis=0),
                                        rows[:, b, :], None, bounds_check=E * CAP - 1, oob_is_err=False).then_inc(dispatched, 16)

            add_base(0, 0)
            rstd(0, moments1, vareps1, rstd1_done, mv1, ve1, rstd1)

            def body(g, first=False, last=False):
                for n in range(PAIRS + 1):
                    if n >= 1:
                        m = n - 1
                        after((recip_done, pair(g, n)))
                        for i in range(4):
                            p = pool.tensor_scalar(pr[:, m % 4, i, :], pr[:, m % 4, i, :], rc[:, m % 4, i:i + 1], 1.0, ALU.mult, ALU.mult)
                        p.then_inc(normed, 1)
                    if n in (0, 1):
                        if first and n == 0:
                            after((xn_done, GB))
                        elif n == 0:
                            jobs = Jobs(g)
                            after((xn_done, GB * (g + 1)), *jobs.emptied(jobs.last_before("O", 1)))
                        b = slice(2 * n, 2 * n + 2)
                        pool.tensor_tensor(hx[:, b, :], hraw[:, b, :], xn[:, b, :], ALU.add).then_inc(hx_done, 1)
                    if n == AT_RSTD2 and not first:
                        rstd(g - 1, moments2, vareps2, rstd2_done, mv2, ve2, rstd2)
                    if n in (AT_BASE, AT_BASE + 1) and not last:
                        add_base(g + 1, n - AT_BASE)
                    if n == AT_RSTD1 and not last:
                        rstd(g + 1, moments1, vareps1, rstd1_done, mv1, ve1, rstd1)
                if not first:
                    for i in range(TOPK * GB):
                        dispatch(g - 1, i)

            body(0, first=True)
            with pool.Fori(1, G - 1) as g:
                body(g)
            body(G - 1, last=True)
            rstd(G - 1, moments2, vareps2, rstd2_done, mv2, ve2, rstd2)
            for i in range(TOPK * GB):
                dispatch(G - 1, i)

            def w2_low(e):
                stage = stage_b[:, :].rearrange("p (c n) -> p c n", c=MC)
                for k in range(4):
                    c = slice(2 * k, 2 * k + 2)
                    after((w2_hi_done, 4 * e + k + 1))
                    pool.tensor_tensor(w2_lo[:, c, :], stage[:, c, :], w2_hi[:, c, :].bitcast(F32), ALU.subtract).then_inc(w2_lo_done, 1)

            def add_results(e):
                for t in range(CT):
                    after((y_done, CT * e + t + 1))
                    if t == 0:
                        if isinstance(e, int) and e == 0:
                            after((slots_cleared, 16 * (E + 1)))
                        else:
                            after((added, 16 * CT * e))
                    pool.tensor_scalar(yout[:, t, :], ysum[:, t, :], gate[:, t:t + 1], 1.0, ALU.mult, ALU.mult).then_inc(gated, 1)
                    after((gated, CT * e + t + 1))
                    pool.indirect_dma_start(out, bass.IndirectOffsetOnAxis(ap=dest[:, t:t + 1], axis=0),
                                            yout[:, t, :], None, compute_op=ALU.add).then_inc(added, 16)

            attention_over(pool)
            w2_low(0)
            add_results(0)
            with pool.Fori(1, E) as e:
                w2_low(e)
                add_results(e)

        @block.scalar
        def _(act):
            act.dma_start(b1_raw[:, :], b1.rearrange("e (m p) -> (e m) p", p=128)).then_inc(b1_in, 16)
            def drain(jobs, name, k, dst, src, **kw):
                act.wait_ge(filled, jobs.filled(name, k))
                act.activation(dst, src, ACT.Copy, **kw).then_inc(act_drained, 1)

            def drain_x(jobs, k):
                drain(jobs, "X", k, xT_hi[:, k, :], jobs.bank("X", k)[:, 0:GT])

            def drain_k(jobs, c):
                drain(jobs, "K", c, kT[0:DK, c % 2, :, 0, :], jobs.bank("K", c)[0:DK, 0:GT].rearrange("p (b t) -> p b t", b=GB))

            def drain_v(jobs, b):
                drain(jobs, "V", 2 * b, vv[:, b, 0:512], jobs.bank("V", 2 * b)[0:T, :])

            def drain_y(jobs):
                drain(jobs, "Y", 0, x2T[:, 0, :], jobs.bank("Y", 0)[:, 0:GT])

            jobs = Jobs("start")
            for k in range(4):
                drain(jobs, "W", k, embW[:, 2 * k:2 * k + 2, :], jobs.bank("W", k)[0:2 * PR, :].rearrange("p (j d) -> p j d", j=2))
            act.dma_start(stage_a[:, :].rearrange("p (c n) -> p c n", c=KC), Wv.rearrange("(c p) n -> p c n", p=128)).then_inc(stage_a_in, 16)
            act.dma_start(router_sb[:, :, :], router_w.rearrange("(c p) e -> p c e", p=128)).then_inc(small_in, 16)
            act.dma_start(router_bb[:, :, :], router_b.rearrange("(o b e) -> o b e", o=1, b=1).broadcast_to([T, GB, E])).then_inc(small_in, 16)
            act.wait_ge(base_zero, 2)
            act.dma_start(base[0:1 + NP, :], pos_enc[0, :, :]).then_inc(small_in, 16)
            act.dma_start(brow[1:1 + NP, :], tok_b.rearrange("(o d) -> o d", o=1).broadcast_to([NP, D])).then_inc(small_in, 16)
            act.wait_ge(stage_a_in, 16)
            act.activation(wqkv_hi[:, :, 2 * HD:], stage_a[:, :].rearrange("p (c n) -> p c n", c=KC), ACT.Copy).then_inc(stage_a_hi, 1)
            act.wait_ge(stage_b_in, 16)
            act.activation(wqkv_hi[:, :, 0:HD], stage_b[:, :].rearrange("p (c n) -> p c n", c=KC), ACT.Copy).then_inc(stage_b_hi, 1)
            act.wait_ge(stage_a_lo, 1)
            act.dma_start(stage_a[:, :].rearrange("p (c n) -> p c n", c=KC), Wk.rearrange("(c p) n -> p c n", p=128)).then_inc(stage_a_in, 16)
            act.wait_ge(stage_a_in, 32)
            act.activation(wqkv_hi[:, :, HD:2 * HD], stage_a[:, :].rearrange("p (c n) -> p c n", c=KC), ACT.Copy).then_inc(stage_a_hi, 1)
            for k in range(KC):
                drain_x(jobs, k)
            for b in range(GB):
                drain_v(jobs, b)
            act.wait_ge(key_pad, 1)
            drain_k(jobs, 0)

            def router_exp(k):
                act.wait_ge(routed, ROUTE_STEPS * k + ROUTE_PARTS[0])
                act.activation(ex[:, :, :], ls[:, :, :], ACT.Exp).then_inc(lexp_done, 1)

            def body(g, first=False, last=False):
                jobs = Jobs(g)
                for n in range(PAIRS + 3):
                    if 1 <= n <= LAST_QK and n % 2 == 1:
                        drain_k(jobs, n // 2 + 1)
                    if not first and n == AT_Y + 1:
                        drain_y(jobs)
                    if not last:
                        if n == AT_X:
                            for k in range(KC):
                                drain_x(jobs, k)
                        for b in V_FIRST.get(n - 1, ()):
                            drain_v(jobs, b)
                    if 3 <= n:
                        m = n - 3
                        c, b = m // 2, 2 * (m % 2)
                        if first and m == 0:
                            act.wait_ge(slots_cleared, 16 * (E + 1))
                        act.wait_ge(o_done, pair(g, m + 1))
                        act.activation(oT_hi[:, c, b * T:(b + 2) * T], o_bank[m % 2][:, 0:2 * T], ACT.Copy).then_inc(o_hi, 1)
                    if 2 <= n < PAIRS + 2:
                        m = n - 2
                        act.wait_ge(pT_done, pair(g, m + 1))
                        act.activation(pT[:, m % 2, :, :], pT_bank[0:T, 0:4 * T].rearrange("p (i q) -> p i q", i=4), ACT.Copy).then_inc(pT_copied, 1)
                    if n < PAIRS:
                        act.wait_ge(bias_done, pair(g, n + 1))
                        if not (first and n < 4):
                            act.wait_ge(pT_done, pair(g, n - 3))
                        for i in range(4):
                            a = act.activation(pr[:, n % 4, i, :], sm[:, n % 2, i, :], ACT.Exp, bias=nb[:, n % 2, i:i + 1],
                                               scale=SCALE, accum_out=rs[:, n % 4, i:i + 1])
                        a.then_inc(exp_done, 1)
                    if not first and n == AT_L + 2:
                        router_exp(g - 1)
                    if first and n - WO_AT in range(WO_PARTS):
                        if n == WO_AT:
                            act.wait_ge(stage_b_in, 32)
                        c = slice(2 * (n - WO_AT), 2 * (n - WO_AT) + 2)
                        act.activation(wo_hi[:, c, :], stage_b[:, :].rearrange("p (c n) -> p c n", c=HP)[:, c, :], ACT.Copy).then_inc(stage_b_hi, 1)
                if not last:
                    drain_k(jobs, 0)

            body(0, first=True)
            with act.Fori(1, G - 1) as g:
                body(g)
            body(G - 1, last=True)
            drain_y(Jobs("end"))
            router_exp(G - 1)

            def split_w1(k):
                c = slice(k % 2 * 512, k % 2 * 512 + 512)
                act.activation(w1_hi[:, k // 2, c], stage_a[:, :].rearrange("p (c n) -> p c n", c=KC)[:, k // 2, c], ACT.Copy).then_inc(w1_hi_done, 1)

            def split_w2(e, k):
                if k == 0:
                    act.wait_ge(w2_in, 16 * e + 16)
                    if not (isinstance(e, int) and e == 0):
                        act.wait_ge(e_filled, e_count(e, -1))
                c = slice(2 * k, 2 * k + 2)
                act.activation(w2_hi[:, c, :], stage_b[:, :].rearrange("p (c n) -> p c n", c=MC)[:, c, :], ACT.Copy).then_inc(w2_hi_done, 1)

            def drain_slots(e, first=False):
                for i, (k, (t0, nt)) in enumerate(XJOBS):
                    j = NF + i
                    act.wait_ge(e_filled, i + 1 if first else e_count(e - 1, j))
                    act.activation(xsT_hi[:, k, t0 * T:(t0 + nt) * T], ebank(j)[:, 0:nt * T], ACT.Copy).then_inc(xs_hi, 1)

            def first_layer(e, first=False):
                for j in range(NF):
                    i, m = divmod(j, MC)
                    if j in (1, 3, 5, 7):
                        split_w2(e, j // 2)
                    waits = [(e_filled, e_count(e, j))]
                    if not (first and j < 4):
                        waits.append((hid_done, NF * e + (j - 3)))
                    wait_apart(act, *waits)
                    act.activation(gl[:, j % 4, 0:SPLIT_N[i]], ebank(j)[:, 0:SPLIT_N[i]], ACT.Gelu,
                                   bias=b1T[:, bass.ds(MC * e + m, 1)]).then_inc(gelu_done, 1)

            def next_w1(e):
                act.wait_ge(w1_in, 16 * (e + 2))
                for k in range(4):
                    split_w1(k)

            attention_over(act)
            act.wait_ge(w1_in, 16)
            for k in range(4):
                split_w1(k)
            drain_slots(0, first=True)

            def expert(e, first=False, last=False):
                first_layer(e, first)
                if not last:
                    drain_slots(e + 1)
                    next_w1(e)

            expert(0, first=True)
            with act.Fori(1, E - 1) as e:
                expert(e)
            expert(E - 1, last=True)

        @block.vector
        def _(dve):
            def split_low(lo, whole, hi, done):
                dve.tensor_tensor(lo, whole, hi.bitcast(F32), ALU.subtract).then_inc(done, 1)

            def drain(jobs, name, k, dst, src):
                dve.wait_ge(filled, jobs.filled(name, k))
                dve.tensor_copy(dst, src).then_inc(dve_drained, 1)

            def drain_x(jobs, k):
                dve.wait_ge(filled, jobs.filled("X", k))
                dve.wait_ge(act_drained, jobs.total(jobs.index("X", k), "a"))
                split_low(xT_lo[:, k, :], jobs.bank("X", k)[:, 0:GT], xT_hi[:, k, :], dve_drained)

            def drain_q(jobs, c):
                drain(jobs, "Q", c, qT[:, c % 2, :], jobs.bank("Q", c)[:, 0:GT])

            def drain_k(jobs, c):
                drain(jobs, "K", c, kT[DK:128, c % 2, :, 1, :], jobs.bank("K", c)[DK:128, 0:GT].rearrange("p (b t) -> p b t", b=GB))

            def drain_v(jobs, b):
                drain(jobs, "V", 2 * b + 1, vv[:, b, 512:1024], jobs.bank("V", 2 * b + 1)[0:T, :])

            def drain_o(jobs, g, k):
                dve.wait_ge(filled, jobs.filled("O", k))
                if not (isinstance(g, int) and g == 0):
                    dve.wait_ge(out_set, 16 * g)
                dve.tensor_tensor(h2[:, 2 * k:2 * k + 2, :], jobs.bank("O", k)[0:T, :].rearrange("p (b d) -> p b d", b=2),
                                  hx[:, 2 * k:2 * k + 2, :], ALU.add).then_inc(dve_drained, 1)

            def statistics(b, src, st, stats):
                dve.bn_stats(st[:, b, :], src[:, b, :]).then_inc(stats, 1)

            def moments(k, st, mv, stats, done):
                wait_apart(dve, (stats, GB * k + GB))
                for b in range(GB):
                    i = dve.bn_aggr(mv[:, b, :], st[:, b, :])
                i.then_inc(done, 1)

            def normalise(b, dst, src, mv, rstd, done):
                dve.tensor_scalar(dst, src, mv[:, b, 0:1], rstd[:, b:b + 1], ALU.subtract, ALU.mult).then_inc(done, 1)

            def drain_embedded(g):
                dve.wait_ge(embedded, g + 1)
                dve.tensor_copy(embT[:, :, :], score_bank[0][:, 0:KC * GB * NP].rearrange("p (k t) -> p k t", k=KC)).then_inc(embT_done, 1)

            def drain_e(jobs):
                drain(jobs, "E", 0, emb[:, :, :], jobs.bank("E", 0)[0:2 * NP, :].rearrange("p (k d) -> p k d", k=2))

            dve.memset(kT[:, :, :, :, :], 0.0).then_inc(key_pad, 1)
            jobs = Jobs("start")
            drain(jobs, "B", 0, b1T[:, :], jobs.bank("B", 0)[:, 0:E * MC])
            dve.wait_ge(stage_a_hi, 1)
            split_low(wqkv_lo[:, :, 2 * HD:], stage_a[:, :].rearrange("p (c n) -> p c n", c=KC), wqkv_hi[:, :, 2 * HD:], stage_a_lo)
            drain_embedded(0)
            drain_e(jobs)
            dve.wait_ge(stage_b_hi, 1)
            split_low(wqkv_lo[:, :, 0:HD], stage_b[:, :].rearrange("p (c n) -> p c n", c=KC), wqkv_hi[:, :, 0:HD], stage_b_lo)
            dve.wait_ge(tokens_in, TOKENS)
            dve.wait_ge(consts_done, CONSTS)
            dve.tensor_tensor(hraw[:, 2:GB, :], hraw[:, 2:GB, :], base[:, None, :].broadcast_to([T, 2, D]), ALU.add).then_inc(first_based, 1)
            dve.wait_ge(first_based, 1)
            for b in (2, 3):
                statistics(b, hraw, st1, stats1)
            dve.wait_ge(based, 1)
            for b in (0, 1):
                statistics(b, hraw, st1, stats1)
            moments(0, st1, mv1, stats1, moments1)
            dve.wait_ge(rstd1_done, 1)
            for b in range(GB):
                normalise(b, xn[:, b, :], hraw[:, b, :], mv1, rstd1, xn_done)
            for k in range(KC):
                drain_x(jobs, k)
            dve.wait_ge(stage_a_hi, 2)
            split_low(wqkv_lo[:, :, HD:2 * HD], stage_a[:, :].rearrange("p (c n) -> p c n", c=KC), wqkv_hi[:, :, HD:2 * HD], stage_a_lo)
            for b in range(GB):
                drain_v(jobs, b)
            drain_embedded(1)
            drain_q(jobs, 0)
            dve.wait_ge(key_pad, 1)
            drain_k(jobs, 0)
            drain_q(jobs, 1)
            dve.wait_ge(consts_done, CONSTS)

            def over_experts(ap):
                return ap[:, :, None].broadcast_to([T, GB, E])

            def route(jobs, k, part):
                at = [ROUTE_STEPS * k + sum(ROUTE_PARTS[:part])]
                made = [0]

                def step(ins):
                    ins.then_inc(routed, 1)
                    made[0] += 1

                def latest():
                    dve.wait_ge(routed, at[0] + made[0])

                if part == 0:
                    dve.wait_ge(filled, jobs.filled("L", 0))
                    dve.tensor_tensor(lg[:, :, :], jobs.bank("L", 0)[0:T, 0:GB * E].rearrange("p (b e) -> p b e", e=E),
                                      router_bb[:, :, :], ALU.add).then_inc(dve_drained, 1)
                    dve.wait_ge(dve_drained, jobs.drained("L", 0)[0][1])
                    step(dve.tensor_reduce(lmax[:, :], lg[:, :, :], AX.X, ALU.max))
                    latest()
                    step(dve.tensor_tensor(ls[:, :, :], lg[:, :, :], over_experts(lmax), ALU.subtract))
                if part == 1:
                    step(dve.tensor_copy(rows[:, :, ID:ID + 1].rearrange("p b o -> p (b o)"), tokid[:, :]))
                    latest()
                    step(dve.tensor_scalar(tokid[:, :], tokid[:, :], float(GT), None, ALU.add))
                    dve.wait_ge(lexp_done, k + 1)
                    step(dve.tensor_reduce(es[:, :], ex[:, :, :], AX.X, ALU.add))
                    latest()
                    step(dve.reciprocal(er[:, :], es[:, :]))
                    latest()
                    step(dve.tensor_tensor(rows[:, :, GATE0:GATE0 + E], ex[:, :, :], over_experts(er), ALU.mult))
                    latest()
                if part in (2, 3):
                    i = part - 2
                    gates = rows[:, :, GATE0:GATE0 + E] if i == 0 else g2[:, :, :]
                    if i == 1:
                        step(dve.scalar_tensor_tensor(out=g2[:, :, :], in0=oh[:, 0], scalar=-2.0, in1=rows[:, :, GATE0:GATE0 + E],
                                                      op0=ALU.mult, op1=ALU.add))
                        latest()
                    step(dve.tensor_reduce(gmax[:, :], gates, AX.X, ALU.max))
                    latest()
                    step(dve.tensor_tensor(eq[:, :, :], gates, over_experts(gmax), ALU.is_equal))
                    latest()
                    step(dve.tensor_tensor(te[:, :, :], eq[:, :, :], io8[:, :, :], ALU.mult))
                    latest()
                    step(dve.tensor_reduce(pick[:, i, :], te[:, :, :], AX.X, ALU.min))
                    latest()
                    step(dve.tensor_tensor(oh[:, i], io8[:, :, :], over_experts(pick[:, i, :]), ALU.is_equal))
                    latest()
                if part == 4:
                    step(dve.tensor_tensor(chosen[:, :, :], oh[:, 0], oh[:, 1], ALU.add))
                    for b in range(GB):
                        latest()
                        step(dve.tensor_tensor(before[:, b + 1, :], before[:, b, :], chosen[:, b, :], ALU.add))
                if part == 5:
                    dve.wait_ge(filled, jobs.filled("C", 0))
                    step(dve.tensor_copy(before[:, 0, :], before[:, GB, :]))
                    dve.tensor_tensor(po_[:, :, :, :], oh[:, :, :, :], jobs.bank("C", 0)[0:T, 0:GB * E].rearrange("p (o b e) -> p o b e", o=1, e=E).broadcast_to([T, TOPK, GB, E]),
                                      ALU.mult).then_inc(dve_drained, 1)
                    dve.wait_ge(dve_drained, jobs.drained("C", 0)[0][1])
                    step(dve.tensor_reduce(ps_[:, :, :], po_[:, :, :, :], AX.X, ALU.add))
                    latest()
                    step(dve.scalar_tensor_tensor(out=sl0[:, :, :], in0=pick[:, :, :], scalar=float(CAP), in1=ps_[:, :, :],
                                                  op0=ALU.mult, op1=ALU.add))
                    step(dve.tensor_scalar(over[:, :, :], ps_[:, :, :], float(CAP), OUT_OF_RANGE, ALU.is_gt, ALU.mult))
                    latest()
                    step(dve.scalar_tensor_tensor(out=slot[:, :, :], in0=sl0[:, :, :], scalar=float(E * CAP - 1), in1=over[:, :, :],
                                                  op0=ALU.add, op1=ALU.add))
                assert made[0] == ROUTE_PARTS[part], (part, made)

            def normalise_rows(k, b):
                dve.wait_ge(rstd2_done, k + 1)
                normalise(b, rows[:, b, 0:D], h2[:, b, :], mv2, rstd2, xn2_done)

            def body(g, first=False, last=False):
                jobs = Jobs(g)
                for n in range(PAIRS + 3):
                    if 1 <= n <= LAST_QK:
                        name, c = next_qk(n - 1)
                        (drain_k if name == "K" else drain_q)(jobs, c)
                    if not last and n == AT_E + 1:
                        drain_e(jobs)
                    if not first and n == AT_Y + 1:
                        drain(jobs, "Y", 1, x2T[:, 1, :], jobs.bank("Y", 1)[:, 0:GT])
                    if not first and n == AT_L + 1:
                        route(jobs, g - 1, 0)
                    if not last and n == AT_X:
                        for k in range(KC):
                            drain_x(jobs, k)
                    if n < PAIRS:
                        wait_apart(dve, (scores_done, pair(g, n + 1)))
                        for i in range(4):
                            m = dve.tensor_tensor_reduce(sm[:, n % 2, i, :], score_bank[n % 2][0:T, i * T:(i + 1) * T], mask[:, :],
                                                         1.0, NEG, ALU.add, ALU.max, mx[:, n % 2, i:i + 1])
                        m.then_inc(max_done, 1)
                        dve.wait_ge(max_done, pair(g, n + 1))
                        dve.tensor_scalar(nb[:, n % 2, :], mx[:, n % 2, :], -SCALE, None, ALU.mult).then_inc(bias_done, 1)
                    if 1 <= n <= PAIRS:
                        dve.wait_ge(exp_done, pair(g, n))
                        dve.reciprocal(rc[:, (n - 1) % 4, :], rs[:, (n - 1) % 4, :]).then_inc(recip_done, 1)
                    if 3 <= n:
                        m = n - 3
                        c, b = m // 2, 2 * (m % 2)
                        dve.wait_ge(o_hi, pair(g, m + 1))
                        split_low(oT_lo[:, c, b * T:(b + 2) * T], o_bank[m % 2][:, 0:2 * T], oT_hi[:, c, b * T:(b + 2) * T], o_lo)
                    if first and n - 1 - WO_AT in range(WO_PARTS):
                        c = slice(2 * (n - 1 - WO_AT), 2 * (n - WO_AT))
                        dve.wait_ge(stage_b_hi, 1 + n - WO_AT)
                        split_low(wo_lo[:, c, :], stage_b[:, :].rearrange("p (c n) -> p c n", c=HP)[:, c, :], wo_hi[:, c, :], stage_b_lo)
                    if not first:
                        for b in STATS2.get(n, ()):
                            statistics(b, h2, st2, stats2)
                        if n == MOMENTS2:
                            moments(g - 1, st2, mv2, stats2, moments2)
                        for b in NORM2.get(n, ()):
                            normalise_rows(g - 1, b)
                        if n in ROUTE_AT:
                            route(jobs, g - 1, ROUTE_AT[n])
                    if not last:
                        if n in STATS1:
                            dve.wait_ge(based, 2 * g + 3)
                        for b in STATS1.get(n, ()):
                            statistics(b, hraw, st1, stats1)
                        if n == MOMENTS1:
                            moments(g + 1, st1, mv1, stats1, moments1)
                        if n in NORM1:
                            dve.wait_ge(rstd1_done, g + 2)
                            dve.wait_ge(hx_done, 2 * g + 2)
                        for b in NORM1.get(n, ()):
                            normalise(b, xn[:, b, :], hraw[:, b, :], mv1, rstd1, xn_done)
                        for b in V_SECOND.get(n, ()):
                            drain_v(jobs, b)
                if not last and not (isinstance(g, int) and g == G - 2):
                    drain_embedded(g + 2)
                if not first:
                    route(jobs, g - 1, 5)
                for k in range(2):
                    drain_o(jobs, g, k)
                    if last:
                        dve.wait_ge(dve_drained, jobs.total(jobs.index("O", k), "d"))
                        for b in (2 * k, 2 * k + 1):
                            statistics(b, h2, st2, stats2)
                if not last:
                    drain_q(jobs, 0)
                    drain_k(jobs, 0)
                    drain_q(jobs, 1)
                if not first:
                    wait_apart(dve, (dispatched, 16 * TOPK * GB * g))

            body(0, first=True)
            with dve.Fori(1, G - 2) as g:
                body(g)
            body(G - 2)
            body(G - 1, last=True)
            jobs = Jobs("end")
            moments(G - 1, st2, mv2, stats2, moments2)
            for b in range(GB):
                normalise_rows(G - 1, b)
            drain(jobs, "Y", 1, x2T[:, 1, :], jobs.bank("Y", 1)[:, 0:GT])
            for part in range(6):
                route(jobs, G - 1, part)

            def w1_low(e):
                for k in range(4):
                    c = slice(k % 2 * 512, k % 2 * 512 + 512)
                    dve.wait_ge(w1_hi_done, 4 * e + k + 1)
                    split_low(w1_lo[:, k // 2, c], stage_a[:, :].rearrange("p (c n) -> p c n", c=KC)[:, k // 2, c], w1_hi[:, k // 2, c], w1_lo_done)

            def drain_slots(e):
                for i, (k, (t0, nt)) in enumerate(XJOBS):
                    dve.wait_ge(xs_hi, NX * e + i + 1)
                    split_low(xsT_lo[:, k, t0 * T:(t0 + nt) * T], ebank(NF + i)[:, 0:nt * T],
                              xsT_hi[:, k, t0 * T:(t0 + nt) * T], xs_done)

            def first_layer(e, first=False):
                for j in range(NF):
                    i, m = divmod(j, MC)
                    s, w = SPLIT_N[0] * i, SPLIT_N[i]
                    if j == 6:
                        if not first:
                            wait_apart(dve, (added, 16 * CT * e))
                        dve.tensor_copy(gate[:, :], xs[:, :, bass.ds(GATE0 + e, 1)].rearrange("p t o -> p (t o)")).then_inc(meta_done, 1)
                        dve.tensor_copy(dest[:, :], xs[:, :, ID:ID + 1].rearrange("p t o -> p (t o)")).then_inc(meta_done, 1)
                    dve.wait_ge(gelu_done, NF * e + j + 1)
                    dve.tensor_copy(hid_hi[:, m, s:s + w], gl[:, j % 4, 0:w]).then_inc(hid_hi_done, 1)
                    dve.wait_ge(hid_hi_done, NF * e + j + 1)
                    split_low(hid_lo[:, m, s:s + w], gl[:, j % 4, 0:w], hid_hi[:, m, s:s + w], hid_done)

            def second_layer(e, last=False):
                for t in range(CT):
                    j = NF + NX + t
                    dve.wait_ge(e_filled, e_count(e, j, last))
                    dve.tensor_tensor(ysum[:, t, :], ebank(j)[0:T, 0:D],
                                      b2b[:, bass.ds(e, 1), :].rearrange("p o d -> p (o d)"), ALU.add).then_inc(y_done, 1)

            def expert(e, first=False, last=False):
                first_layer(e, first)
                if not last:
                    drain_slots(e + 1)
                    w1_low(e + 1)
                second_layer(e, last)

            attention_over(dve)
            w1_low(0)
            drain_slots(0)
            dve.wait_ge(b2_in, 16)
            dve.wait_ge(slots_in, 16)
            expert(0, first=True)
            with dve.Fori(1, E - 1) as e:
                expert(e)
            expert(E - 1, last=True)

        @block.tensor
        def _(pe):
            def claim(jobs, name, k):
                wait_all(pe, jobs.bank_free(name, k))
                return jobs.bank(name, k)

            def embed(g):
                pe.wait_ge(pix_in, 32 * (g + 1))
                if not (isinstance(g, int) and g < 2):
                    pe.wait_ge(max_done, pair(g - 1, 0))
                elif g == 1:
                    pe.wait_ge(embT_done, 1)
                tokens = pix[:, :, :, :].rearrange("p b n w -> p (b n w)").rearrange("p (t j) -> p t j", j=PX)
                for k in range(KC):
                    for j in range(HPX):
                        m = pe.matmul(score_bank[0][:, k * GB * NP:(k + 1) * GB * NP], embW[:, j, k * 128:(k + 1) * 128], tokens[:, :, j],
                                      start=(j == 0), stop=(j == HPX - 1))
                m.then_inc(embedded, 1)

            def transpose_patches(jobs, g):
                pe.wait_ge(embT_done, g + 1)
                dst = claim(jobs, "E", 0)
                for i in range(2):
                    for k in range(KC):
                        o = i * D + k * 128
                        m = pe.transpose(dst[0:2 * NP, o:o + 128], embT[:, k, i * 2 * NP:(i + 1) * 2 * NP], ident[:, :])
                m.then_inc(filled, 1)

            def transpose_tokens(jobs, name, src, k):
                dst = claim(jobs, name, k)
                for b in range(GB):
                    m = pe.transpose(dst[:, b * T:(b + 1) * T], src[:, b, k * 128:(k + 1) * 128], ident[0:T, 0:T])
                m.then_inc(filled, 1)

            def project(jobs, name, c):
                dst = claim(jobs, name, c)[:, 0:GT]
                col = (0 if name == "Q" else HD) + c * 128
                for k in range(KC):
                    m = halves(dst, (wqkv_hi[:, k, col:col + 128], wqkv_lo[:, k, col:col + 128]),
                               (xT_hi[:, k, :], xT_lo[:, k, :]), k == 0, k == KC - 1, pe)
                m.then_inc(filled, 1)

            def project_v(jobs, i):
                b, half = divmod(i, 2)
                if i == 0:
                    wait_all(pe, jobs.drained("X", KC - 1))
                    dst = jobs.bank("V", i)[0:T, :]
                else:
                    dst = claim(jobs, "V", i)[0:T, :]
                col = 2 * HD + half * 512
                for k in range(KC):
                    m = halves(dst, (xT_hi[:, k, b * T:(b + 1) * T], xT_lo[:, k, b * T:(b + 1) * T]),
                               (wqkv_hi[:, k, col:col + 512], wqkv_lo[:, k, col:col + 512]), k == 0, k == KC - 1, pe)
                m.then_inc(filled, 1)

            def project_o(jobs, i):
                dst = claim(jobs, "O", i)
                for b in (2 * i, 2 * i + 1):
                    for c in range(HP):
                        m = halves(dst[0:T, (b % 2) * D:(b % 2 + 1) * D],
                                   (oT_hi[:, c, b * T:(b + 1) * T], oT_lo[:, c, b * T:(b + 1) * T]),
                                   (wo_hi[:, c, :], wo_lo[:, c, :]), c == 0, c == HP - 1, pe)
                m.then_inc(filled, 1)

            jobs = Jobs("start")
            pe.wait_ge(ident_done, 1)
            pe.wait_ge(tokW_in, 16)
            for k in range(4):
                dst = claim(jobs, "W", k)
                for j in (2 * k, 2 * k + 1):
                    for dc in range(KC):
                        src = tok_raw[:, dc, :].rearrange("p (r j) -> p j r", j=HPX)[:, j]
                        o = (j % 2) * D + dc * 128
                        m = pe.transpose(dst[0:2 * PR, o:o + 128], src, ident[:, :])
                m.then_inc(filled, 1)
            pe.wait_ge(b1_in, 16)
            dst = claim(jobs, "B", 0)
            pe.transpose(dst[:, 0:E * MC], b1_raw[:, :], ident[0:E * MC, 0:E * MC]).then_inc(filled, 1)
            wait_all(pe, jobs.drained("W", 3))
            embed(0)
            transpose_patches(jobs, 0)
            for k in range(KC):
                pe.wait_ge(xn_done, GB)
                transpose_tokens(jobs, "X", xn, k)
            pe.wait_ge(stage_a_lo, 1)
            for i in range(2 * GB):
                project_v(jobs, i)
            embed(1)
            pe.wait_ge(stage_b_lo, 1)
            project(jobs, "Q", 0)
            pe.wait_ge(stage_a_lo, 2)
            project(jobs, "K", 0)
            project(jobs, "Q", 1)
            pe.wait_ge(consts_done, CONSTS)
            pe.wait_ge(small_in, SMALL)
            pe.wait_ge(key_pad, 1)

            def scores(g, n, jobs, first):
                c, b0 = n // 2, 2 * (n % 2)
                if b0 == 0:
                    wait_all(pe, jobs.emptied(jobs.last_before("K", 0) if c == 0 else jobs.index("K", c)))
                if n == 0 and not (isinstance(g, int) and g == G - 1):
                    pe.wait_ge(embT_done, g + 2)
                elif not (first and n < 2):
                    pe.wait_ge(max_done, pair(g, n - 1))
                for b in range(2):
                    m = pe.matmul(score_bank[n % 2][0:T, b * 2 * T:(b + 1) * 2 * T], qT[:, c % 2, (b0 + b) * T:(b0 + b + 1) * T],
                                  kT[:, c % 2, b0 + b, :, :], start=True, stop=True)
                m.then_inc(scores_done, 1)

            def transpose_probs(g, n, first):
                pe.wait_ge(normed, pair(g, n + 1))
                if not (first and n < 1):
                    pe.wait_ge(pT_copied, pair(g, n))
                for i in range(4):
                    m = pe.transpose(pT_bank[0:T, i * T:(i + 1) * T], pr[:, n % 4, i, :], ident[0:T, 0:T])
                m.then_inc(pT_done, 1)

            def weigh_values(g, n, first):
                c, b0 = n // 2, 2 * (n % 2)
                pe.wait_ge(pT_copied, pair(g, n + 1))
                if not (first and n < 2):
                    pe.wait_ge(o_lo, pair(g, n - 1))
                for b in range(2):
                    for h in range(2):
                        v0 = (2 * c + h) * DK
                        m = pe.matmul(o_bank[n % 2][h * DK:(h + 1) * DK, b * T:(b + 1) * T], vv[:, b0 + b, v0:v0 + DK], pT[:, n % 2, 2 * b + h, :],
                                      start=True, stop=True)
                m.then_inc(o_done, 1)

            def logits(jobs):
                if jobs.index("Y", 1) + len(bank) > jobs.index("L", 0):
                    wait_all(pe, jobs.drained("Y", 0) + jobs.drained("Y", 1))
                    dst = jobs.bank("L", 0)
                else:
                    dst = claim(jobs, "L", 0)
                for b in range(GB):
                    for c in range(KC):
                        m = pe.matmul(dst[0:T, b * E:(b + 1) * E], x2T[:, c, b * T:(b + 1) * T], router_sb[:, c, :], start=(c == 0), stop=(c == KC - 1))
                m.then_inc(filled, 1)

            def count_places(jobs, k):
                pe.wait_ge(routed, ROUTE_STEPS * k + sum(ROUTE_PARTS[:5]))
                dst = claim(jobs, "C", 0)[0:T, 0:GB * E]
                pe.matmul(dst, upto[:, :], chosen[:, :, :], start=True, stop=False)
                pe.matmul(dst, ones[:, :], before[:, 0:GB, :], start=False, stop=True).then_inc(filled, 1)

            def body(g, first=False, last=False):
                jobs = Jobs(g)
                for k in (2 * GB - 2, 2 * GB - 1):
                    wait_all(pe, jobs.emptied(jobs.last_before("V", k)))
                for n in range(PAIRS + 3):
                    if not last and n == AT_X:
                        pe.wait_ge(xn_done, GB * (g + 2))
                        for k in range(KC):
                            transpose_tokens(jobs, "X", xn, k)
                    if n < PAIRS:
                        scores(g, n, jobs, first)
                    if 3 <= n:
                        weigh_values(g, n - 3, first)
                    if 2 <= n < PAIRS + 2:
                        transpose_probs(g, n - 2, first)
                    if n < LAST_QK:
                        project(jobs, *next_qk(n))
                    if not last:
                        if n == AT_E:
                            transpose_patches(jobs, g + 1)
                    if not first:
                        if n == AT_Y:
                            pe.wait_ge(xn2_done, GB * g)
                            for k in range(KC):
                                transpose_tokens(jobs, "Y", rows, k)
                        if n == AT_L:
                            logits(jobs)
                    if not last:
                        for b in V_FIRST.get(n, ()):
                            project_v(jobs, 2 * b)
                        for b in V_SECOND.get(n, ()):
                            project_v(jobs, 2 * b + 1)
                if not last and not (isinstance(g, int) and g == G - 2):
                    embed(g + 2)
                if not first:
                    count_places(jobs, g - 1)
                if first:
                    pe.wait_ge(stage_b_lo, 1 + WO_PARTS)
                pe.wait_ge(o_lo, pair(g, PAIRS))
                for k in range(2):
                    project_o(jobs, k)
                if not last:
                    project(jobs, "Q", 0)
                    project(jobs, "K", 0)
                    project(jobs, "Q", 1)

            body(0, first=True)
            with pe.Fori(1, G - 2) as g:
                body(g)
            body(G - 2)
            body(G - 1, last=True)
            jobs = Jobs("end")
            pe.wait_ge(xn2_done, GB * G)
            for k in range(KC):
                transpose_tokens(jobs, "Y", rows, k)
            logits(jobs)
            count_places(jobs, G - 1)

            def wait_bank(e, j, first=False, last=False):
                i = j - EB
                if last and i >= NF:
                    i -= EB
                if i < 0 and first:
                    if i + EB > 0:
                        pe.wait_ge(xs_done, i + EB)
                elif i < 0:
                    pe.wait_ge(y_done, CT * e + (i + 1))
                elif i < NF:
                    pe.wait_ge(gelu_done, NF * e + i + 1)
                elif i < NF + NX:
                    pe.wait_ge(xs_done, NX * (e + 1) + (i - NF + 1))

            def transpose_slots(e, first=False):
                pe.wait_ge(slots_in, 16 * (e + 1))
                for i, (k, (t0, nt)) in enumerate(XJOBS):
                    if not first:
                        wait_bank(e - 1, NF + i)
                    for t in range(nt):
                        m = pe.transpose(ebank(NF + i)[:, t * T:(t + 1) * T], xs[:, t0 + t, k * 128:(k + 1) * 128], ident[0:T, 0:T])
                    m.then_inc(e_filled, 1)

            def first_layer(e, first=False):
                wait_apart(pe, (w1_lo_done, 4 * (e + 1)))
                for j in range(NF):
                    if j in (0, MC):
                        xs_wait = NX * e + (KC if j == 0 else NX)
                        if j == 0 or first:
                            pe.wait_ge(xs_done, xs_wait)
                    i, m_ = divmod(j, MC)
                    wait_bank(e, j, first)
                    s, w = SPLIT_N[0] * i, SPLIT_N[i]
                    for k in range(KC):
                        m = halves(ebank(j)[:, 0:w], (w1_hi[:, k, m_ * 128:(m_ + 1) * 128], w1_lo[:, k, m_ * 128:(m_ + 1) * 128]),
                                   (xsT_hi[:, k, s:s + w], xsT_lo[:, k, s:s + w]), k == 0, k == KC - 1, pe)
                    m.then_inc(e_filled, 1)

            def second_layer(e, last=False):
                wait_apart(pe, (w2_lo_done, 4 * (e + 1)))
                for t in range(CT):
                    j = NF + NX + t
                    if t in (0, FIRST_TILES):
                        pe.wait_ge(hid_done, NF * e + (MC if t == 0 else NF))
                    wait_bank(e, j, last=last)
                    for m_ in range(MC):
                        m = halves(ebank(j)[0:T, 0:D], (hid_hi[:, m_, t * T:(t + 1) * T], hid_lo[:, m_, t * T:(t + 1) * T]),
                                   (w2_hi[:, m_, :], w2_lo[:, m_, :]), m_ == 0, m_ == MC - 1, pe)
                    m.then_inc(e_filled, 1)

            def expert(e, first=False, last=False):
                first_layer(e, first)
                if not last:
                    transpose_slots(e + 1)
                second_layer(e, last)

            transpose_slots(0, first=True)
            expert(0, first=True)
            with pe.Fori(1, E - 1) as e:
                expert(e)
            expert(E - 1, last=True)


_INS = ["x", "txt", "L0_tok_W", "L0_tok_b", "L0_tok_cls_token", "L0_tok_pos_enc", "L0_attn_Wq", "L0_attn_Wk",
        "L0_attn_Wv", "L0_attn_Wo", "L0_ffn_router_w", "L0_ffn_router_b", "L0_ffn_w1", "L0_ffn_b1", "L0_ffn_w2",
        "L0_ffn_b2"]


def kernel(**inputs):
    import numpy as np
    import concourse.bacc as bacc
    from concourse.bass_utils import run_bass_kernel_spmd

    nc = bacc.Bacc("TRN2", target_bir_lowering=False, num_devices=1)
    arrays, args = {}, []
    for name in _INS:
        a = np.ascontiguousarray(inputs[name])
        arrays[f"in_{name}_dram"] = a
        args.append(nc.dram_tensor(f"in_{name}_dram", a.shape, mybir.dt.from_np(a.dtype), kind="ExternalInput").ap())
    out = nc.dram_tensor("out_dram", (B * T + CAP, D), F32, kind="ExternalOutput").ap()
    slots = nc.dram_tensor("slots_dram", (E * CAP, ROW), F32).ap()
    build(nc, *args, out, slots)
    r = run_bass_kernel_spmd(nc, [arrays], core_ids=[0])
    return r.results[0]["out_dram"][0:B * T].reshape(B, T, D)
```
